# Optimizing a Trainium2 kernel written in Bass

```python
import numpy as np
import jax
import jax.numpy as jnp

def _softmax(x, axis=-1):
    return jax.nn.softmax(x, axis=axis)

def _gelu(x):
    return jax.nn.gelu(x, approximate=True)

def _silu(x):
    return jax.nn.silu(x)

def _sigmoid(x):
    return jax.nn.sigmoid(x)

def _layernorm(x, axis=-1, eps=1e-05):
    m = jnp.mean(x, axis=axis, keepdims=True)
    v = jnp.var(x, axis=axis, keepdims=True)
    return (x - m) / jnp.sqrt(v + eps)

def _scatter_add(tgt, idx, src, axis=0):
    return tgt.at[idx].add(src)

def _segment_sum(src, seg, n):
    return jax.ops.segment_sum(src, seg, n)
kernel_name = 'mk_vit_tower_cls_d1_tok_img512_r4_bdc53b'

def setup_inputs(seed: int=0):
    np.random.seed(seed)
    _w = jnp.asarray

    def _rec_inputs():
        import jax
        import jax.numpy as jnp
        _rk = jax.random.key(seed)
        x = -0.000356955 + 1 * jax.random.normal(jax.random.fold_in(_rk, 1), (16, 3, 96, 96), jnp.float32)
        cls_tok = 0.02 * jax.random.normal(jax.random.fold_in(_rk, 5), (1, 1, 128), jnp.float32)
        return (x, cls_tok)
    x, cls_tok = _rec_inputs()

    def _L0_tok_setup():
        import jax, jax.numpy as jnp
        import numpy as np
        key = jax.random.key(seed)
        k1, k2, k3 = jax.random.split(key, 3)
        B, C, H, W = (128, 3, 224, 224)
        E, p = (128, 16)
        K = C * p * p
        img = jax.random.normal(k1, (B, C, H, W), dtype=jnp.float32)
        w = jax.random.normal(k2, (E, K), dtype=jnp.float32) * (1.0 / np.sqrt(K))
        b = jax.random.normal(k3, (E,), dtype=jnp.float32)
        return {'img': img, 'w': w, 'b': b, 'patch_size': p}
    _L0_tok_all = _L0_tok_setup()
    _L0_tok_in = {k: v for k, v in _L0_tok_all.items() if k in ('w', 'b')}
    del _L0_tok_all

    def _L0_attn_setup():
        import jax, jax.numpy as jnp
        import numpy as np
        B, S, D = (8, 512, 128)
        HEADS = 8
        DEPTH = D // HEADS
        SCALE = DEPTH ** (-0.5)
        LN_EPS = 0.001
        key = jax.random.key(seed)
        ks = jax.random.split(key, 9)

        def w(k, shape, scale=0.02):
            return jax.random.normal(k, shape, dtype=jnp.float32) * scale
        return {'x': jax.random.normal(ks[0], (B, S, D), dtype=jnp.float32), 'Wq': w(ks[1], (D, D)), 'bq': jnp.zeros((D,), jnp.float32), 'Wk': w(ks[2], (D, D)), 'bk': jnp.zeros((D,), jnp.float32), 'Wv': w(ks[3], (D, D)), 'bv': jnp.zeros((D,), jnp.float32), 'Wo': w(ks[4], (D, D)), 'bo': jnp.zeros((D,), jnp.float32), 'gamma': jnp.ones((D,), jnp.float32), 'beta': jnp.zeros((D,), jnp.float32)}
    _L0_attn_all = _L0_attn_setup()
    _L0_attn_in = {k: v for k, v in _L0_attn_all.items() if k in ('Wq', 'bq', 'Wk', 'bk', 'Wv', 'bv', 'Wo', 'bo', 'gamma', 'beta')}
    del _L0_attn_all

    def _L0_ffn_setup():
        import jax, jax.numpy as jnp
        import numpy as np
        B, L, H, E, F, C = (8, 2048, 128, 8, 256, 2)
        key = jax.random.key(seed)
        ks = jax.random.split(key, 4)
        x = jax.random.normal(ks[0], (B, L, H), jnp.float32)
        Wg = jax.random.normal(ks[1], (H, E), jnp.float32) * H ** (-0.5)
        W1 = jax.random.normal(ks[2], (E, H, F), jnp.float32) * H ** (-0.5)
        b1 = jnp.zeros((E, F), jnp.float32)
        W2 = jax.random.normal(ks[3], (E, F, H), jnp.float32) * F ** (-0.5)
        b2 = jnp.zeros((E, H), jnp.float32)
        return {'x': x, 'Wg': Wg, 'W1': W1, 'b1': b1, 'W2': W2, 'b2': b2}
    _L0_ffn_all = _L0_ffn_setup()
    _L0_ffn_in = {k: v for k, v in _L0_ffn_all.items() if k in ('Wg', 'W1', 'b1', 'W2', 'b2')}
    del _L0_ffn_all
    return {'x': x, 'cls_tok': cls_tok, 'L0_tok_w': _L0_tok_in['w'], 'L0_tok_b': _L0_tok_in['b'], 'L0_attn_Wq': _L0_attn_in['Wq'], 'L0_attn_bq': _L0_attn_in['bq'], 'L0_attn_Wk': _L0_attn_in['Wk'], 'L0_attn_bk': _L0_attn_in['bk'], 'L0_attn_Wv': _L0_attn_in['Wv'], 'L0_attn_bv': _L0_attn_in['bv'], 'L0_attn_Wo': _L0_attn_in['Wo'], 'L0_attn_bo': _L0_attn_in['bo'], 'L0_attn_gamma': _L0_attn_in['gamma'], 'L0_attn_beta': _L0_attn_in['beta'], 'L0_ffn_Wg': _L0_ffn_in['Wg'], 'L0_ffn_W1': _L0_ffn_in['W1'], 'L0_ffn_b1': _L0_ffn_in['b1'], 'L0_ffn_W2': _L0_ffn_in['W2'], 'L0_ffn_b2': _L0_ffn_in['b2']}

def reference(x, cls_tok, L0_tok_w, L0_tok_b, L0_attn_Wq, L0_attn_bq, L0_attn_Wk, L0_attn_bk, L0_attn_Wv, L0_attn_bv, L0_attn_Wo, L0_attn_bo, L0_attn_gamma, L0_attn_beta, L0_ffn_Wg, L0_ffn_W1, L0_ffn_b1, L0_ffn_W2, L0_ffn_b2):
    import jax
    import jax.numpy as jnp

    def _L0_tok_ref(img, w, b, patch_size):
        import jax, jax.numpy as jnp
        import numpy as np
        B, C, H, W = img.shape
        p = patch_size
        Hp, Wp = (H // p, W // p)
        S = Hp * Wp
        patches = img.reshape(B, C, Hp, p, Wp, p)
        patches = patches.transpose(0, 2, 4, 1, 3, 5).reshape(B, S, C * p * p)
        out = jnp.einsum('bsk,ek->bse', patches, w) + b
        return out

    def _L0_attn_ref(x, Wq, bq, Wk, bk, Wv, bv, Wo, bo, gamma, beta):
        import jax, jax.numpy as jnp
        import numpy as np
        B, S, D = (8, 512, 128)
        HEADS = 8
        DEPTH = D // HEADS
        SCALE = DEPTH ** (-0.5)
        LN_EPS = 0.001
        q = jax.nn.relu(x @ Wq + bq) * SCALE
        k = jax.nn.relu(x @ Wk + bk)
        v = jax.nn.relu(x @ Wv + bv)
        scores = jnp.einsum('bsd,btd->bst', q, k)
        attn = jax.nn.softmax(scores, axis=-1)
        ctx = jnp.einsum('bst,btd->bsd', attn, v)
        out = jax.nn.relu(ctx @ Wo + bo)
        mu = jnp.mean(out, axis=-1, keepdims=True)
        var = jnp.var(out, axis=-1, keepdims=True)
        return (out - mu) * jax.lax.rsqrt(var + LN_EPS) * gamma + beta

    def _L0_ffn_ref(x, Wg, W1, b1, W2, b2):
        import jax, jax.numpy as jnp
        import numpy as np
        B, L, H, E, F, C = (8, 2048, 128, 8, 256, 2)
        b, l, h = x.shape
        e = Wg.shape[1]
        k = min(max(int(l * C / e), 1), l)
        S = jax.nn.softmax(x @ Wg, axis=-1)
        St = jnp.swapaxes(S, 1, 2)
        G, I = jax.lax.top_k(St, k)
        ex = jnp.take_along_axis(x[:, None], I[..., None], axis=2)
        hmid = jax.nn.gelu(jnp.einsum('bekh,ehf->bekf', ex, W1) + b1[None, :, None, :], approximate=False)
        out = jnp.einsum('bekf,efh->bekh', hmid, W2) + b2[None, :, None, :]
        vals = G[..., None] * out
        new_x = jnp.zeros_like(x).at[jnp.arange(b)[:, None, None], I].add(vals)
        return new_x
    h = _L0_tok_ref(x, L0_tok_w, L0_tok_b, 16)
    h = jnp.concatenate([jnp.broadcast_to(cls_tok, (h.shape[0], 1, h.shape[2])), h], axis=1)
    h = h + _L0_attn_ref(_layernorm(h, axis=-1), L0_attn_Wq, L0_attn_bq, L0_attn_Wk, L0_attn_bk, L0_attn_Wv, L0_attn_bv, L0_attn_Wo, L0_attn_bo, L0_attn_gamma, L0_attn_beta)
    h = h + _L0_ffn_ref(_layernorm(h, axis=-1), L0_ffn_Wg, L0_ffn_W1, L0_ffn_b1, L0_ffn_W2, L0_ffn_b2)
    return h

_drawn_inputs = setup_inputs


def setup_inputs(seed=0):
    import zlib

    import numpy as np

    out = dict(_drawn_inputs(seed))
    spreads = {'L0_attn_bq': (0.0, 0.8),
     'L0_attn_bk': (0.0, 0.8),
     'L0_attn_bv': (0.0, 0.1),
     'L0_attn_bo': (0.0, 0.1),
     'L0_attn_gamma': (1.0, 0.2),
     'L0_attn_beta': (0.0, 0.1),
     'L0_ffn_b1': (0.0, 0.527),
     'L0_ffn_b2': (0.0, 0.382)}
    factors = {'cls_tok': 6.506, 'L0_attn_Wq': 8.0, 'L0_attn_Wk': 8.0}
    for name, (base, spread) in spreads.items():
        noise = np.random.default_rng([zlib.crc32(name.encode()), seed]).standard_normal(out[name].shape)
        drawn = base * np.exp(spread * noise) if base else spread * noise
        out[name] = jnp.asarray(drawn.astype(out[name].dtype))
    for name, factor in factors.items():
        out[name] = (out[name] * factor).astype(out[name].dtype)
    return out
```

```python
import numpy as np
import concourse.bass as bass
from concourse import mybir
from contextlib import ExitStack

B, C, IMG, PATCH, D = 16, 3, 96, 16, 128
HP = IMG // PATCH
S = HP * HP + 1
KCH = C * PATCH * PATCH // 128
E, F = 8, 256
FCH = F // 128
TOPK = min(max(int(S * 2 / E), 1), S)
SCALE = 16 ** -0.5
EPS_PRE, EPS_ATTN = 1e-5, 1e-3

TILE_B = 3
TILES = -(-B // TILE_B)
NB = [min(TILE_B, B - TILE_B * t) for t in range(TILES)]
NT = [n * S for n in NB]
P = TILE_B * S
SL = TILE_B * TOPK
GROUP_T = 3
GROUPS = TILES // GROUP_T
NS = [sum(NB[GROUP_T * g:GROUP_T * (g + 1)]) * TOPK for g in range(GROUPS)]
EH = E // 2
BANK = 512
EC_PER_BANK = 6
EC_BANKS = -(-E * FCH // EC_PER_BANK)
MASK_OFF = -2.0 ** 100

I_TOK, I_CLS, I_Q, I_K, I_V, I_O, I_B1 = range(7)
I_B2 = I_B1 + E * FCH
ITEMS = I_B2 + E

C_ID, C_PART, C_IOTA, C_FEND = 0, 128, 131, 131 + SL
H_SEL, H_TOK, H_ML, H_MR, H_END = 0, ITEMS, ITEMS + P, ITEMS + 2 * P, ITEMS + 3 * P


def constants():
    cf = np.zeros((128, C_FEND), np.float32)
    cf[:, C_ID:C_ID + 128] = np.eye(128)
    for p in range(3 * ITEMS):
        cf[p, C_PART + p % 3] = SCALE if p // 3 == I_Q else 1.0
    cf[:, C_IOTA:C_IOTA + SL] = np.arange(1, SL + 1)
    ch = np.zeros((128, H_END), np.float32)
    for p in range(3 * ITEMS):
        ch[p, H_SEL + p // 3] = 1.0
    tok = np.arange(P)
    for s in range(3):
        ch[3 * I_TOK + s, H_TOK:H_TOK + P] = tok % S != 0
        ch[3 * I_CLS + s, H_TOK:H_TOK + P] = tok % S == 0
    for b in range(TILE_B):
        ch[b, H_ML:H_ML + P] = tok // S == b
        ch[b, H_MR:H_MR + P] = np.where(tok // S == b, 0.0, MASK_OFF)
    return cf, ch


def vit_block(nc, patches, w_tok, bias_rows, const_f, const_h, w_qkvo, w_gate, gamma, beta, w1, w2, out):
    f32, bf16 = mybir.dt.float32, mybir.dt.bfloat16
    ALU, ACT, AX = mybir.AluOpType, mybir.ActivationFunctionType, mybir.AxisListType

    ctx = ExitStack()
    with ctx:
        def sb(name, shape, dt=f32):
            return ctx.enter_context(nc.sbuf_tensor(name, shape, dt))

        def sem(name):
            return ctx.enter_context(nc.semaphore(name))

        xp = [sb(f"xp{t}", [128, KCH * NT[t]]) for t in range(TILES)]
        wt = sb("wt", [128, KCH * D])
        braw = sb("braw", [128, D])
        bhi, bmid = sb("bhi", [128, D], bf16), sb("bmid", [128, D], bf16)
        bres1, bres2 = sb("bres1", [128, D]), sb("bres2", [128, D])
        bsum1, bsum2 = sb("bsum1", [128, D]), sb("bsum2", [128, D])
        biases = sb("biases", [128, D], bf16)
        cf = sb("cf", [128, C_FEND])
        chf = sb("chf", [128, H_END])
        ch = sb("ch", [128, H_END], bf16)
        wqkvo = sb("wqkvo", [128, 4 * D])
        wqs = sb("wqs", [128, D])
        wg = sb("wg", [128, E])
        gam, bet = sb("gam", [P, D]), sb("bet", [P, D])
        w1s = sb("w1s", [128, E, F])
        w2s = sb("w2s", [128, E, FCH, D])

        stats = sb("stats", [P, TILES, 3, 6])
        mv = sb("mv", [P, TILES, 3, 2])
        vareps, rstd, power = sb("vareps", [P, TILES, 3]), sb("rstd", [P, TILES, 3]), sb("power", [P, 1])
        hn, hb, hnT = sb("hn", [P, TILES, D]), sb("hb", [P, TILES, D]), sb("hnT", [128, TILES, P])
        qk = sb("qk", [128, TILES, 2 * P])
        v = sb("v", [P, TILES, D])
        nmax, esum, erec = sb("nmax", [P, TILES]), sb("esum", [P, TILES]), sb("erec", [P, TILES])
        prob, attn = sb("prob", [P, TILES, P]), sb("attn", [P, TILES, P])
        attnT, ctxT = sb("attnT", [P, TILES, P]), sb("ctxT", [128, TILES, P])
        o, og, h1 = sb("o", [P, TILES, D]), sb("og", [P, TILES, D]), sb("h1", [P, TILES, D])
        xn, xnT = sb("xn", [P, TILES, D]), sb("xnT", [128, TILES, P])
        gnmax, gexp = sb("gnmax", [P, TILES]), sb("gexp", [P, TILES, E])
        gsum, grec = sb("gsum", [P, TILES]), sb("grec", [P, TILES])
        G = sb("G", [P, TILES, E])
        R = GROUP_T * E
        GT = [sb(f"GT{g}", [R, P]) for g in range(GROUPS)]
        top8 = [sb(f"top8_{g}", [R, TILE_B, 8]) for g in range(GROUPS)]
        ninth = [sb(f"ninth{g}", [R, TILE_B, 8]) for g in range(GROUPS)]
        left8 = [sb(f"left8_{g}", [R, P]) for g in range(GROUPS)]
        left9 = [sb(f"left9_{g}", [R, P]) for g in range(GROUPS)]
        chosen = [sb(f"chosen{g}", [R, P]) for g in range(GROUPS)]
        count = [sb(f"count{g}", [R, P]) for g in range(GROUPS)]
        slotT = [sb(f"slotT{g}", [R, P]) for g in range(GROUPS)]
        slot = [sb(f"slot{g}", [P, R]) for g in range(GROUPS)]
        pick = [sb(f"pick{g}", [P, R * SL]) for g in range(GROUPS)]
        wpick = [sb(f"wpick{g}", [P, R * SL]) for g in range(GROUPS)]
        exT = [sb(f"exT{g}", [128, E, NS[g]]) for g in range(GROUPS)]
        hid = [sb(f"hid{g}", [128, E * FCH, NS[g]]) for g in range(GROUPS)]
        yT = [sb(f"yT{g}", [128, R * SL]) for g in range(GROUPS)]
        y = [sb(f"y{g}", [EH * SL, GROUP_T * 2, D]) for g in range(GROUPS)]
        put = [sb(f"put{g}", [EH * SL, GROUP_T * 2, P]) for g in range(GROUPS)]
        res = sb("res", [P, TILES, D])
        warm = sb("warm", [1, 8])

        bank = [ctx.enter_context(nc.psum_tensor(f"bank{i}", [128, BANK], f32)) for i in range(8)]

        in_x = [sem(f"in_x{t}") for t in range(TILES)]
        in_wt, in_bias, in_cf, in_ch, in_qkvo, in_wg = (sem(n) for n in (
            "in_wt", "in_bias", "in_cf", "in_ch", "in_qkvo", "in_wg"))
        in_gb, in_w1, in_w2, out_done = sem("in_gb"), sem("in_w1"), sem("in_w2"), sem("out_done")
        dve_done = sem("dve_done")
        biases_ready, ch_ready, wqs_ready = sem("biases_ready"), sem("ch_ready"), sem("wqs_ready")
        fills_ready = sem("fills_ready")
        mv_ready = [sem(f"mv_ready{i}") for i in range(3)]
        vareps_ready = [sem(f"vareps_ready{i}") for i in range(3)]
        rstd_ready = [sem(f"rstd_ready{i}") for i in range(3)]
        power_ready = sem("power_ready")
        h_mm, hn_ready, h_used = sem("h_mm"), sem("hn_ready"), sem("h_used")
        hnT_mm, hnT_sb, qk_mm, qk_sb, v_mm, v_sb = (sem(n) for n in (
            "hnT_mm", "hnT_sb", "qk_mm", "qk_sb", "v_mm", "v_sb"))
        s_mm, nmax_ready, prob_ready, attn_ready = (sem(n) for n in ("s_mm", "nmax_ready", "prob_ready", "attn_ready"))
        attnT_mm, attnT_sb, ctx_mm, ctx_sb = (sem(n) for n in ("attnT_mm", "attnT_sb", "ctx_mm", "ctx_sb"))
        o_mm, o_sb, xn_ready, xnT_mm, xnT_sb = (sem(n) for n in ("o_mm", "o_sb", "xn_ready", "xnT_mm", "xnT_sb"))
        lg_mm, gnmax_ready, gexp_ready = sem("lg_mm"), sem("gnmax_ready"), sem("gexp_ready")
        G_ready, GT_mm, slotT_ready, slot_mm, pick_ready = (sem(n) for n in (
            "G_ready", "GT_mm", "slotT_ready", "slot_mm", "pick_ready"))
        wpick_ready, ex_mm, ex_sb = sem("wpick_ready"), sem("ex_mm"), sem("ex_sb")
        hid_mm, hid_sb, y_mm, yT_sb = sem("hid_mm"), sem("hid_sb"), sem("y_mm"), sem("yT_sb")
        yt_mm, y_sb, put_mm, put_sb = sem("yt_mm"), sem("y_sb"), sem("put_mm"), sem("put_sb")
        res_mm, res_ready = sem("res_mm"), sem("res_ready")

        ident = cf[:, C_ID:C_ID + 128]

        def sel(item, n):
            return ch[:, H_SEL + item:H_SEL + item + 1].broadcast_to([128, n])

        def sel_blocks(item, k, n):
            return ch[:, H_SEL + item:H_SEL + item + k].unsqueeze(2).broadcast_to([128, k, n])

        def group(t):
            return t // GROUP_T, t % GROUP_T

        def blocks(g):
            return [(i, GROUP_T * g + i) for i in range(GROUP_T)]

        def spans(g):
            full = sum(NB[GROUP_T * g + i] == TILE_B for i in range(GROUP_T))
            return [(0, full, SL)] + [(i, 1, NB[GROUP_T * g + i] * TOPK) for i in range(full, GROUP_T)]

        def slot_cols(buf, i, k, w):
            return buf[:, i * E * SL:i * E * SL + k * E * w].rearrange("p (r w) -> p r w", w=w)

        def half_cols(i, h, w):
            return slice(i * E * SL + h * EH * w, i * E * SL + (h + 1) * EH * w)

        def ec_blocks(n):
            return [(k, min(EC_PER_BANK, E * FCH - k)) for k in range(0, E * FCH, EC_PER_BANK)][n]

        block = ctx.enter_context(nc.Block())

        @block.sync
        def _(sp):
            sp.dma_start(braw[:, :], bias_rows).then_inc(in_bias, 16)
            sp.dma_start(wt[:, :], w_tok).then_inc(in_wt, 16)
            sp.dma_start(xp[0][:, :], patches[:, 0:KCH * NT[0]]).then_inc(in_x[0], 16)
            sp.dma_start(cf[:, :], const_f).then_inc(in_cf, 16)
            sp.dma_start(wqkvo[:, :], w_qkvo).then_inc(in_qkvo, 16)
            for t in range(1, TILES):
                at = KCH * sum(NT[:t])
                sp.dma_start(xp[t][:, :], patches[:, at:at + KCH * NT[t]]).then_inc(in_x[t], 16)
            sp.dma_start(w1s[:, :, :], w1).then_inc(in_w1, 16)
            sp.dma_start(w2s[:, :, :, :], w2).then_inc(in_w2, 16)
            for t in range(TILES):
                sp.wait_ge(res_ready, t + 1)
                at = sum(NT[:t])
                sp.dma_start(out[at:at + NT[t], :], res[0:NT[t], t, :]).then_inc(out_done, 16)
            sp.wait_ge(out_done, 16 * TILES)

        @block.gpsimd
        def _(pool):
            nc.gpsimd.memset(gexp[:, :, :], 0.0).then_inc(fills_ready, 1)
            nc.gpsimd.memset(gsum[:, :], 1.0).then_inc(fills_ready, 1)
            for g in range(GROUPS):
                nc.gpsimd.memset(ninth[g][:, :, :], -1.0).then_inc(fills_ready, 1)
            nc.gpsimd.memset(power[:, :], -0.5).then_inc(power_ready, 1)
            pool.wait_ge(power_ready, 1)

            def inv_std(t, which, eps):
                pool.wait_ge(mv_ready[which], t + 1)
                nc.gpsimd.tensor_scalar(vareps[0:NT[t], t, which:which + 1], mv[0:NT[t], t, which, 1:2],
                                        eps, None, ALU.add).then_inc(vareps_ready[which], 1)
                pool.wait_ge(vareps_ready[which], t + 1)
                nc.gpsimd.tensor_tensor(rstd[0:NT[t], t, which:which + 1], vareps[0:NT[t], t, which:which + 1],
                                        power[0:NT[t], :], ALU.pow).then_inc(rstd_ready[which], 1)

            for step in range(TILES + 2):
                if step < TILES:
                    inv_std(step, 0, EPS_PRE)
                if 0 <= step - 2 < TILES:
                    inv_std(step - 2, 1, EPS_ATTN)
                    inv_std(step - 2, 2, EPS_PRE)
            for g in range(GROUPS):
                pool.wait_ge(pick_ready, g + 1)
                for i, k, w in spans(g):
                    last = nc.gpsimd.tensor_tensor(
                        slot_cols(wpick[g], i, k, w), slot_cols(pick[g], i, k, w),
                        G[:, GROUP_T * g + i:GROUP_T * g + i + k, :].rearrange("p t e -> p (t e)").unsqueeze(2)
                        .broadcast_to([P, k * E, w]), ALU.mult)
                last.then_inc(wpick_ready, 1)

        @block.scalar
        def _(act):
            act.dma_start(chf[:, :], const_h).then_inc(in_ch, 16)
            act.dma_start(gam[:, :], gamma.partition_broadcast(P)).then_inc(in_gb, 16)
            act.dma_start(bet[:, :], beta.partition_broadcast(P)).then_inc(in_gb, 16)
            act.dma_start(wg[:, :], w_gate).then_inc(in_wg, 16)

            def hnT_copy(t):
                act.wait_ge(hnT_mm, t + 1)
                nc.scalar.activation(hnT[:, t, 0:NT[t]], bank[2][:, 0:NT[t]], ACT.Copy).then_inc(hnT_sb, 1)

            def v_relu(t):
                act.wait_ge(v_mm, t + 1)
                nc.scalar.activation(v[0:NT[t], t, :], bank[2][0:NT[t], 128:256], ACT.Relu).then_inc(v_sb, 1)

            def softmax_exp(t):
                act.wait_ge(nmax_ready, t + 1)
                nc.scalar.activation(prob[0:NT[t], t, 0:NT[t]], bank[4][0:NT[t], 0:NT[t]], ACT.Exp,
                                     bias=nmax[0:NT[t], t:t + 1],
                                     accum_out=esum[0:NT[t], t:t + 1]).then_inc(prob_ready, 1)

            def attnT_copy(t):
                act.wait_ge(attnT_mm, t + 1)
                nc.scalar.activation(attnT[0:NT[t], t, 0:NT[t]], bank[5][0:NT[t], 0:NT[t]],
                                     ACT.Copy).then_inc(attnT_sb, 1)

            def ctx_copy(t):
                act.wait_ge(ctx_mm, t + 1)
                nc.scalar.activation(ctxT[:, t, 0:NT[t]], bank[5][:, 128:128 + NT[t]], ACT.Copy).then_inc(ctx_sb, 1)

            def o_relu(t):
                act.wait_ge(o_mm, t + 1)
                nc.scalar.activation(o[0:NT[t], t, :], bank[6][0:NT[t], 0:D], ACT.Relu).then_inc(o_sb, 1)

            def xnT_copy(t):
                act.wait_ge(xnT_mm, t + 1)
                nc.scalar.activation(xnT[:, t, 0:NT[t]], bank[6][:, 128:128 + NT[t]], ACT.Copy).then_inc(xnT_sb, 1)

            def gate_exp(t):
                act.wait_ge(gnmax_ready, t + 1)
                if t == 0:
                    act.wait_ge(fills_ready, 2)
                nc.scalar.activation(gexp[0:NT[t], t, :], bank[7][0:NT[t], E * t:E * t + E], ACT.Exp,
                                     bias=gnmax[0:NT[t], t:t + 1],
                                     accum_out=gsum[0:NT[t], t:t + 1]).then_inc(gexp_ready, 1)

            for step in range(TILES + 2):
                if 0 <= step - 1 < TILES:
                    softmax_exp(step - 1)
                if 0 <= step - 2 < TILES:
                    o_relu(step - 2)
                if step < TILES:
                    hnT_copy(step)
                if 0 <= step - 1 < TILES:
                    attnT_copy(step - 1)
                if 0 <= step - 2 < TILES:
                    xnT_copy(step - 2)
                if step < TILES:
                    v_relu(step)
                if 0 <= step - 1 < TILES:
                    ctx_copy(step - 1)
                if 0 <= step - 2 < TILES:
                    gate_exp(step - 2)

            def ffn1_gelu(g):
                for n in range(EC_BANKS):
                    k0, k = ec_blocks(n)
                    act.wait_ge(hid_mm, EC_BANKS * g + n + 1)
                    nc.scalar.activation(hid[g][:, k0:k0 + k, :].rearrange("p k n -> p (k n)"),
                                         bank[3 + n][:, 0:k * NS[g]], ACT.Gelu).then_inc(hid_sb, 1)

            def put_copy(g):
                for n, (a, b) in enumerate(((0, 4), (4, 6))):
                    act.wait_ge(put_mm, 2 * g + n + 1)
                    for i in range(a, b):
                        t = GROUP_T * g + i // 2
                        last = nc.scalar.activation(
                            put[g][0:EH * NB[t] * TOPK, i, 0:NT[t]],
                            bank[3 + n][0:EH * NB[t] * TOPK, (i - a) * P:(i - a) * P + NT[t]], ACT.Copy)
                    last.then_inc(put_sb, 1)

            for g in range(GROUPS):
                ffn1_gelu(g)
                put_copy(g)

        @block.vector
        def _(dve):
            done = [0]

            def chain(ins):
                done[0] += 1
                ins.then_inc(dve_done, 1)
                dve.wait_ge(dve_done, done[0])

            def layernorm_stats(src, t, which):
                chain(nc.vector.bn_stats(stats[0:NT[t], t, which, :], src))
                nc.vector.bn_aggr(mv[0:NT[t], t, which, :], stats[0:NT[t], t, which, :]).then_inc(mv_ready[which], 1)
                dve.wait_ge(mv_ready[which], t + 1)

            def normalise(dst, src, t, which):
                return nc.vector.tensor_scalar(dst, src, mv[0:NT[t], t, which, 0:1],
                                               rstd[0:NT[t], t, which:which + 1], ALU.subtract, ALU.mult)

            dve.wait_ge(in_bias, 16)
            chain(nc.vector.tensor_copy(bhi[:, :], braw[:, :]))
            chain(nc.vector.tensor_tensor(bres1[:, :], braw[:, :], bhi[:, :], ALU.subtract))
            chain(nc.vector.tensor_copy(bmid[:, :], bres1[:, :]))
            chain(nc.vector.tensor_tensor(bres2[:, :], bres1[:, :], bmid[:, :], ALU.subtract))
            dve.wait_ge(in_ch, 16)
            nc.vector.tensor_copy(ch[:, :], chf[:, :]).then_inc(ch_ready, 1)
            dve.wait_ge(in_cf, 16)
            chain(nc.vector.tensor_scalar(bsum1[:, :], bhi[:, :], cf[:, C_PART:C_PART + 1], None, ALU.mult))
            chain(nc.vector.scalar_tensor_tensor(bsum2[:, :], bmid[:, :], cf[:, C_PART + 1:C_PART + 2],
                                                 bsum1[:, :], ALU.mult, ALU.add))
            nc.vector.scalar_tensor_tensor(biases[:, :], bres2[:, :], cf[:, C_PART + 2:C_PART + 3],
                                           bsum2[:, :], ALU.mult, ALU.add).then_inc(biases_ready, 1)
            dve.wait_ge(in_qkvo, 16)
            nc.vector.tensor_scalar(wqs[:, :], wqkvo[:, 0:D], SCALE, None, ALU.mult).then_inc(wqs_ready, 1)

            def pre_norm(t):
                dve.wait_ge(h_mm, t + 1)
                h = bank[t % 2][0:NT[t], 0:D]
                layernorm_stats(h, t, 0)
                dve.wait_ge(rstd_ready[0], t + 1)
                normalise(hn[0:NT[t], t, :], h, t, 0).then_inc(hn_ready, 1)
                if t == 0:
                    dve.wait_ge(in_gb, 32)
                nc.vector.tensor_tensor(hb[0:NT[t], t, :], h, bet[0:NT[t], :], ALU.add).then_inc(h_used, 1)

            def qk_relu(t):
                dve.wait_ge(qk_mm, t + 1)
                nc.vector.tensor_scalar(qk[:, t, 0:2 * NT[t]], bank[3][:, 0:2 * NT[t]], 0.0, None,
                                        ALU.max).then_inc(qk_sb, 1)

            def row_max(t):
                dve.wait_ge(s_mm, t + 1)
                nc.vector.tensor_reduce(nmax[0:NT[t], t:t + 1], bank[4][0:NT[t], 0:NT[t]], AX.X, ALU.max,
                                        negate=True).then_inc(nmax_ready, 1)

            def attn_norm(t):
                dve.wait_ge(prob_ready, t + 1)
                chain(nc.vector.reciprocal(erec[0:NT[t], t:t + 1], esum[0:NT[t], t:t + 1]))
                nc.vector.tensor_scalar(attn[0:NT[t], t, 0:NT[t]], prob[0:NT[t], t, 0:NT[t]],
                                        erec[0:NT[t], t:t + 1], None, ALU.mult).then_inc(attn_ready, 1)

            def post_norm(t):
                dve.wait_ge(o_sb, t + 1)
                layernorm_stats(o[0:NT[t], t, :], t, 1)
                chain(nc.vector.scalar_tensor_tensor(og[0:NT[t], t, :], o[0:NT[t], t, :], mv[0:NT[t], t, 1, 0:1],
                                                     gam[0:NT[t], :], ALU.subtract, ALU.mult))
                dve.wait_ge(h_used, t + 1)
                dve.wait_ge(rstd_ready[1], t + 1)
                chain(nc.vector.scalar_tensor_tensor(h1[0:NT[t], t, :], og[0:NT[t], t, :], rstd[0:NT[t], t, 1:2],
                                                     hb[0:NT[t], t, :], ALU.mult, ALU.add))
                layernorm_stats(h1[0:NT[t], t, :], t, 2)
                dve.wait_ge(rstd_ready[2], t + 1)
                normalise(xn[0:NT[t], t, :], h1[0:NT[t], t, :], t, 2).then_inc(xn_ready, 1)

            def gate_max(t):
                dve.wait_ge(lg_mm, t + 1)
                nc.vector.tensor_reduce(gnmax[0:NT[t], t:t + 1], bank[7][0:NT[t], E * t:E * t + E], AX.X, ALU.max,
                                        negate=True).then_inc(gnmax_ready, 1)

            for step in range(TILES + 2):
                if 0 <= step - 1 < TILES:
                    row_max(step - 1)
                if step < TILES:
                    pre_norm(step)
                if 0 <= step - 1 < TILES:
                    attn_norm(step - 1)
                if 0 <= step - 2 < TILES:
                    post_norm(step - 2)
                if step < TILES:
                    qk_relu(step)
                if 0 <= step - 2 < TILES:
                    gate_max(step - 2)

            def gate_probs(g):
                ts = slice(GROUP_T * g, GROUP_T * (g + 1))
                dve.wait_ge(gexp_ready, GROUP_T * (g + 1))
                chain(nc.vector.reciprocal(grec[:, ts], gsum[:, ts]))
                nc.vector.tensor_tensor(G[:, ts, :], gexp[:, ts, :],
                                        grec[:, ts].unsqueeze(2).broadcast_to([P, GROUP_T, E]),
                                        ALU.mult).then_inc(G_ready, 1)

            def top_k(g):
                dve.wait_ge(GT_mm, g + 1)
                chain(nc.vector.tensor_copy(GT[g][:, :], bank[0][0:R, 0:P]))
                for b in range(TILE_B):
                    last = nc.vector.max(top8[g][:, b, :], GT[g][:, b * S:(b + 1) * S])
                chain(last)
                for b in range(TILE_B):
                    last = nc.vector.match_replace(left8[g][:, b * S:(b + 1) * S], top8[g][:, b, :],
                                                   GT[g][:, b * S:(b + 1) * S], -1.0)
                chain(last)
                dve.wait_ge(fills_ready, 2 + GROUPS)
                chain(nc.vector.tensor_reduce(ninth[g][:, :, 0], left8[g][:, :].rearrange("r (b s) -> r b s", b=TILE_B),
                                              AX.X, ALU.max))
                for b in range(TILE_B):
                    last = nc.vector.match_replace(left9[g][:, b * S:(b + 1) * S], ninth[g][:, b, :],
                                                   left8[g][:, b * S:(b + 1) * S], -1.0)
                chain(last)
                chain(nc.vector.tensor_scalar(chosen[g][:, :], left9[g][:, :], 0.0, None, ALU.is_lt))
                chain(nc.vector.tensor_tensor_scan(count[g][:, :], chosen[g][:, :], chosen[g][:, :], 0.0,
                                                   ALU.add, ALU.max))
                nc.vector.tensor_tensor(slotT[g][:, :], count[g][:, :], chosen[g][:, :],
                                        ALU.mult).then_inc(slotT_ready, 1)

            def build_pick(g):
                dve.wait_ge(slot_mm, g + 1)
                chain(nc.vector.tensor_copy(slot[g][:, :], bank[0][0:P, 128:128 + R]))
                for i, k, w in spans(g):
                    last = nc.vector.tensor_tensor(
                        slot_cols(pick[g], i, k, w),
                        slot[g][:, E * i:E * (i + k)].unsqueeze(2).broadcast_to([P, k * E, w]),
                        cf[0:P, C_IOTA:C_IOTA + w].unsqueeze(1).broadcast_to([P, k * E, w]), ALU.is_equal)
                last.then_inc(pick_ready, 1)

            def ex_copy(g):
                dve.wait_ge(ex_mm, g + 1)
                for i, t in blocks(g):
                    n = NB[t] * TOPK
                    last = nc.vector.tensor_copy(
                        exT[g][:, :, i * SL:i * SL + n],
                        bank[1 + i // 2][:, (i % 2) * E * SL:(i % 2) * E * SL + E * n]
                        .rearrange("p (e n) -> p e n", e=E))
                last.then_inc(ex_sb, 1)

            def yT_copy(g):
                for h in range(2):
                    dve.wait_ge(y_mm, 2 * g + h + 1)
                    src = bank[6 + h][:, 0:EH * NS[g]].rearrange("p (e n) -> p e n", e=EH)
                    for i, k, w in spans(g):
                        for j in range(i, i + k):
                            last = nc.vector.tensor_copy(
                                yT[g][:, half_cols(j, h, w)].rearrange("p (e w) -> p e w", e=EH),
                                src[:, :, j * SL:j * SL + w])
                    last.then_inc(yT_sb, 1)

            def y_copy(g):
                for n, (a, b) in enumerate(((0, 4), (4, 6))):
                    dve.wait_ge(yt_mm, 2 * g + n + 1)
                    for i in range(a, b):
                        t = GROUP_T * g + i // 2
                        last = nc.vector.tensor_copy(y[g][0:EH * NB[t] * TOPK, i, :],
                                                     bank[1 + n][0:EH * NB[t] * TOPK, (i - a) * D:(i - a + 1) * D])
                    last.then_inc(y_sb, 1)

            def residual(g):
                for i, t in blocks(g):
                    dve.wait_ge(res_mm, t + 1)
                    nc.vector.tensor_tensor(res[0:NT[t], t, :], bank[0][0:NT[t], i * D:(i + 1) * D],
                                            h1[0:NT[t], t, :], ALU.add).then_inc(res_ready, 1)

            for g in range(GROUPS):
                gate_probs(g)
                top_k(g)
                build_pick(g)
                ex_copy(g)
                yT_copy(g)
                y_copy(g)
                residual(g)

        @block.tensor
        def _(pe):
            def embed(t, part):
                h = bank[t % 2][0:NT[t], 0:D]
                n = NT[t]
                if part == 0:
                    pe.wait_ge(in_x[t], 16)
                    if t == 0:
                        pe.wait_ge(in_wt, 16)
                    if t >= 2:
                        pe.wait_ge(h_used, t - 1)
                for c in range(2 * part, 2 * part + 2):
                    nc.tensor.matmul(h, xp[t][:, c * n:(c + 1) * n], wt[:, c * D:(c + 1) * D],
                                     start=(c == 0), stop=False)
                if part == 2:
                    if t == 0:
                        pe.wait_ge(ch_ready, 1)
                        pe.wait_ge(biases_ready, 1)
                    nc.tensor.matmul(h, ch[:, H_TOK:H_TOK + n], biases[:, :], start=False,
                                     stop=True).then_inc(h_mm, 1)

            def hn_transpose(t):
                pe.wait_ge(hn_ready, t + 1)
                if t == 0:
                    pe.wait_ge(in_cf, 16)
                if t >= 1:
                    pe.wait_ge(v_sb, t)
                nc.tensor.transpose(bank[2][:, 0:NT[t]], hn[0:NT[t], t, :], ident[0:NT[t], 0:NT[t]]).then_inc(hnT_mm, 1)

            def qkv(t):
                n = NT[t]
                pe.wait_ge(hnT_sb, t + 1)
                if t == 0:
                    pe.wait_ge(in_qkvo, 16)
                    pe.wait_ge(wqs_ready, 1)
                if t >= 1:
                    pe.wait_ge(qk_sb, t)
                nc.tensor.matmul(bank[3][:, 0:n], wqs[:, :], hnT[:, t, 0:n], start=True, stop=False)
                nc.tensor.matmul(bank[3][:, 0:n], biases[:, :], sel(I_Q, n), start=False, stop=True)
                nc.tensor.matmul(bank[3][:, n:2 * n], wqkvo[:, D:2 * D], hnT[:, t, 0:n], start=True, stop=False)
                nc.tensor.matmul(bank[3][:, n:2 * n], biases[:, :], sel(I_K, n), start=False,
                                 stop=True).then_inc(qk_mm, 1)
                nc.tensor.matmul(bank[2][0:n, 128:256], hnT[:, t, 0:n], wqkvo[:, 2 * D:3 * D], start=True, stop=False)
                nc.tensor.matmul(bank[2][0:n, 128:256], sel(I_V, n), biases[:, :], start=False,
                                 stop=True).then_inc(v_mm, 1)

            def scores(t):
                n = NT[t]
                pe.wait_ge(qk_sb, t + 1)
                if t >= 1:
                    pe.wait_ge(prob_ready, t)
                s = bank[4][0:n, 0:n]
                nc.tensor.matmul(s, ch[:, H_ML:H_ML + n], ch[:, H_MR:H_MR + n], start=True, stop=False)
                nc.tensor.matmul(s, qk[:, t, 0:n], qk[:, t, n:2 * n], start=False, stop=True).then_inc(s_mm, 1)

            def attn_transpose(t):
                n = NT[t]
                pe.wait_ge(attn_ready, t + 1)
                if t >= 1:
                    pe.wait_ge(ctx_sb, t)
                nc.tensor.transpose(bank[5][0:n, 0:n], attn[0:n, t, 0:n], ident[0:n, 0:n]).then_inc(attnT_mm, 1)

            def context(t):
                n = NT[t]
                pe.wait_ge(attnT_sb, t + 1)
                pe.wait_ge(v_sb, t + 1)
                nc.tensor.matmul(bank[5][:, 128:128 + n], v[0:n, t, :], attnT[0:n, t, 0:n], start=True,
                                 stop=True).then_inc(ctx_mm, 1)

            def project(t):
                n = NT[t]
                pe.wait_ge(ctx_sb, t + 1)
                if t >= 1:
                    pe.wait_ge(xnT_sb, t)
                nc.tensor.matmul(bank[6][0:n, 0:D], ctxT[:, t, 0:n], wqkvo[:, 3 * D:4 * D], start=True, stop=False)
                nc.tensor.matmul(bank[6][0:n, 0:D], sel(I_O, n), biases[:, :], start=False,
                                 stop=True).then_inc(o_mm, 1)

            def xn_transpose(t):
                pe.wait_ge(xn_ready, t + 1)
                nc.tensor.transpose(bank[6][:, 128:128 + NT[t]], xn[0:NT[t], t, :],
                                    ident[0:NT[t], 0:NT[t]]).then_inc(xnT_mm, 1)

            def gate(t):
                pe.wait_ge(xnT_sb, t + 1)
                if t == 0:
                    pe.wait_ge(in_wg, 16)
                if t >= 1:
                    pe.wait_ge(gexp_ready, t)
                nc.tensor.matmul(bank[7][0:NT[t], E * t:E * t + E], xnT[:, t, 0:NT[t]], wg[:, :], start=True,
                                 stop=True).then_inc(lg_mm, 1)

            for part in range(3):
                embed(0, part)
            for step in range(TILES + 2):
                now, prev, old, nxt = step, step - 1, step - 2, step + 1
                if now < TILES:
                    hn_transpose(now)
                if nxt < TILES:
                    embed(nxt, 0)
                if 0 <= prev < TILES:
                    attn_transpose(prev)
                if 0 <= old < TILES:
                    xn_transpose(old)
                if now < TILES:
                    qkv(now)
                if 0 <= prev < TILES:
                    context(prev)
                if nxt < TILES:
                    embed(nxt, 1)
                if 0 <= old < TILES:
                    gate(old)
                if now < TILES:
                    scores(now)
                if 0 <= prev < TILES:
                    project(prev)
                if nxt < TILES:
                    embed(nxt, 2)

            def gates_transpose(g):
                pe.wait_ge(G_ready, g + 1)
                nc.tensor.transpose(bank[0][0:R, 0:P], G[:, GROUP_T * g:GROUP_T * (g + 1), :]
                                    .rearrange("p t e -> p (t e)"), ident[0:P, 0:P]).then_inc(GT_mm, 1)

            def slots_transpose(g):
                pe.wait_ge(slotT_ready, g + 1)
                nc.tensor.transpose(bank[0][0:P, 128:128 + R], slotT[g][:, :], ident[0:R, 0:R]).then_inc(slot_mm, 1)

            def gather(g):
                pe.wait_ge(pick_ready, g + 1)
                for i, t in blocks(g):
                    n = NB[t] * TOPK
                    last = nc.tensor.matmul(bank[1 + i // 2][:, (i % 2) * E * SL:(i % 2) * E * SL + E * n],
                                            xn[0:NT[t], t, :], pick[g][0:NT[t], i * E * SL:i * E * SL + E * n],
                                            start=True, stop=True)
                last.then_inc(ex_mm, 1)

            def ffn1(g):
                n = NS[g]
                pe.wait_ge(ex_sb, g + 1)
                if g == 0:
                    pe.wait_ge(in_w1, 16)
                for k in range(EC_BANKS):
                    k0, kn = ec_blocks(k)
                    if g >= 1:
                        pe.wait_ge(put_sb, 2 * g)
                    nc.tensor.matmul(bank[3 + k][:, 0:kn * n], biases[:, :], sel_blocks(I_B1 + k0, kn, n),
                                     start=True, stop=False, skip_group_check=True)
                    for ec in range(k0, k0 + kn):
                        e, c = ec // FCH, ec % FCH
                        at = (ec - k0) * n
                        last = nc.tensor.matmul(bank[3 + k][:, at:at + n], w1s[:, e, c * 128:(c + 1) * 128],
                                                exT[g][:, e, :], start=False, stop=ec == k0 + kn - 1,
                                                skip_group_check=True)
                    last.then_inc(hid_mm, 1)

            def ffn2(g):
                n = NS[g]
                if g == 0:
                    pe.wait_ge(in_w2, 16)
                pe.wait_ge(hid_sb, EC_BANKS * (g + 1))
                for h in range(2):
                    nc.tensor.matmul(bank[6 + h][:, 0:EH * n], biases[:, :], sel_blocks(I_B2 + EH * h, EH, n),
                                     start=True, stop=False, skip_group_check=True)
                    for i in range(EH):
                        e = EH * h + i
                        for c in range(FCH):
                            last = nc.tensor.matmul(bank[6 + h][:, i * n:(i + 1) * n], w2s[:, e, c, :],
                                                    hid[g][:, FCH * e + c, :], start=False,
                                                    stop=(i == EH - 1 and c == FCH - 1), skip_group_check=True)
                    last.then_inc(y_mm, 1)

            def put_transpose(g):
                pe.wait_ge(wpick_ready, g + 1)
                pe.wait_ge(hid_sb, EC_BANKS * (g + 1))
                for k, (a, b) in enumerate(((0, 4), (4, 6))):
                    for i in range(a, b):
                        t, h = GROUP_T * g + i // 2, i % 2
                        n, w = NT[t], NB[t] * TOPK
                        last = nc.tensor.transpose(
                            bank[3 + k][0:EH * w, (i - a) * P:(i - a) * P + n],
                            wpick[g][0:n, half_cols(i // 2, h, w)], ident[0:n, 0:n])
                    last.then_inc(put_mm, 1)

            def y_transpose(g):
                pe.wait_ge(yT_sb, 2 * (g + 1))
                for k, (a, b) in enumerate(((0, 4), (4, 6))):
                    for i in range(a, b):
                        t, h = GROUP_T * g + i // 2, i % 2
                        w = NB[t] * TOPK
                        last = nc.tensor.transpose(bank[1 + k][0:EH * w, (i - a) * D:(i - a + 1) * D],
                                                   yT[g][:, half_cols(i // 2, h, w)], ident[:, :])
                    last.then_inc(yt_mm, 1)

            def combine(g):
                pe.wait_ge(y_sb, 2 * (g + 1))
                pe.wait_ge(put_sb, 2 * (g + 1))
                for i, t in blocks(g):
                    w = EH * NB[t] * TOPK
                    for h in range(2):
                        last = nc.tensor.matmul(bank[0][0:NT[t], i * D:(i + 1) * D], put[g][0:w, 2 * i + h, 0:NT[t]],
                                                y[g][0:w, 2 * i + h, :], start=h == 0, stop=h == 1)
                    if t % GROUP_T == GROUP_T - 1:
                        last.then_inc(res_mm, GROUP_T)

            for g in range(GROUPS):
                gates_transpose(g)
                slots_transpose(g)
                gather(g)
                ffn1(g)
                ffn2(g)
                put_transpose(g)
                y_transpose(g)
                combine(g)


def kernel(x, cls_tok, L0_tok_w, L0_tok_b, L0_attn_Wq, L0_attn_bq, L0_attn_Wk, L0_attn_bk, L0_attn_Wv, L0_attn_bv,
           L0_attn_Wo, L0_attn_bo, L0_attn_gamma, L0_attn_beta, L0_ffn_Wg, L0_ffn_W1, L0_ffn_b1, L0_ffn_W2, L0_ffn_b2):
    import concourse.bacc as bacc
    from concourse.bass_utils import run_bass_kernel_spmd

    px = np.asarray(x).reshape(B, C, HP, PATCH, HP, PATCH).transpose(1, 3, 5, 0, 2, 4).reshape(KCH, 128, B, S - 1)
    full = np.zeros((KCH, 128, B, S), np.float32)
    full[:, :, :, 1:] = px
    full = full.transpose(1, 0, 2, 3)
    patches = np.concatenate([full[:, :, TILE_B * t:TILE_B * t + NB[t]].reshape(128, KCH * NT[t])
                              for t in range(TILES)], axis=1)
    w_tok = np.asarray(L0_tok_w).reshape(D, KCH, 128).transpose(2, 1, 0).reshape(128, KCH * D)
    rows = np.concatenate([np.asarray(a).reshape(-1, D) for a in (
        L0_tok_b, cls_tok, L0_attn_bq, L0_attn_bk, L0_attn_bv, L0_attn_bo, L0_ffn_b1, L0_ffn_b2)])
    bias_rows = np.zeros((128, D), np.float32)
    bias_rows[0:3 * ITEMS] = np.repeat(rows, 3, axis=0)
    const_f, const_h = constants()
    w_qkvo = np.concatenate([np.asarray(a) for a in (L0_attn_Wq, L0_attn_Wk, L0_attn_Wv, L0_attn_Wo)], axis=1)
    arrays = {
        "patches": patches, "w_tok": w_tok, "bias_rows": bias_rows, "const_f": const_f, "const_h": const_h,
        "w_qkvo": w_qkvo, "w_gate": np.asarray(L0_ffn_Wg), "gamma": np.asarray(L0_attn_gamma),
        "beta": np.asarray(L0_attn_beta), "w1": np.asarray(L0_ffn_W1).transpose(1, 0, 2),
        "w2": np.asarray(L0_ffn_W2).reshape(E, FCH, 128, D).transpose(2, 0, 1, 3),
    }
    arrays = {name: np.ascontiguousarray(a) for name, a in arrays.items()}
    nc = bacc.Bacc("TRN2", target_bir_lowering=False, num_devices=1)
    args = [nc.dram_tensor(name, a.shape, mybir.dt.float32, kind="ExternalInput").ap() for name, a in arrays.items()]
    out = nc.dram_tensor("out", (B * S, D), mybir.dt.float32, kind="ExternalOutput").ap()
    vit_block(nc, *args, out)
    r = run_bass_kernel_spmd(nc, [arrays], core_ids=[0])
    return r.results[0]["out"].reshape(B, S, D)
```

```python
import numpy as np
import concourse.bass as bass
from concourse import mybir
from contextlib import ExitStack

B, C, IMG, PATCH, D = 16, 3, 96, 16, 128
HP = IMG // PATCH
S = HP * HP + 1
KCH = C * PATCH * PATCH // 128
E, F = 8, 256
FCH = F // 128
TOPK = min(max(int(S * 2 / E), 1), S)
SCALE = 16 ** -0.5
EPS_PRE, EPS_ATTN = 1e-5, 1e-3

TILE_B = 3
TILES = -(-B // TILE_B)
NB = [min(TILE_B, B - TILE_B * t) for t in range(TILES)]
NT = [n * S for n in NB]
P = TILE_B * S
SL = TILE_B * TOPK
R = TILES * E
NS = B * TOPK
EH = E // 2
BANK = 512
EC = E * FCH
PER_BANK = BANK // NS
HID_BANKS = -(-EC // PER_BANK)
Y_BANKS = -(-E // PER_BANK)
PAIRS = TILES // 2
WARM_START, WARM_TOPK = 14, 14
MASK_OFF = -2.0 ** 100

I_TOK, I_CLS, I_Q, I_K, I_V, I_O, I_B1 = range(7)
I_B2 = I_B1 + E * FCH
ITEMS = I_B2 + E

C_ID, C_PART, C_IOTA, C_FEND = 0, 128, 131, 131 + SL
H_SEL, H_TOK, H_ML, H_MR, H_END = 0, ITEMS, ITEMS + P, ITEMS + 2 * P, ITEMS + 3 * P


def constants():
    cf = np.zeros((128, C_FEND), np.float32)
    cf[:, C_ID:C_ID + 128] = np.eye(128)
    for p in range(3 * ITEMS):
        cf[p, C_PART + p % 3] = SCALE if p // 3 == I_Q else 1.0
    cf[:, C_IOTA:C_IOTA + SL] = np.arange(1, SL + 1)
    ch = np.zeros((128, H_END), np.float32)
    for p in range(3 * ITEMS):
        ch[p, H_SEL + p // 3] = 1.0
    tok = np.arange(P)
    for s in range(3):
        ch[3 * I_TOK + s, H_TOK:H_TOK + P] = tok % S != 0
        ch[3 * I_CLS + s, H_TOK:H_TOK + P] = tok % S == 0
    for b in range(TILE_B):
        ch[b, H_ML:H_ML + P] = tok // S == b
        ch[b, H_MR:H_MR + P] = np.where(tok // S == b, 0.0, MASK_OFF)
    return cf, ch


def vit_block(nc, patches, w_tok, bias_rows, const_f, const_h, w_qkvo, w_gate, gamma, beta, w1, w2, out):
    f32, bf16 = mybir.dt.float32, mybir.dt.bfloat16
    ALU, ACT, AX = mybir.AluOpType, mybir.ActivationFunctionType, mybir.AxisListType

    ctx = ExitStack()
    with ctx:
        def sb(name, shape, dt=f32):
            return ctx.enter_context(nc.sbuf_tensor(name, shape, dt))

        def sem(name):
            return ctx.enter_context(nc.semaphore(name))

        xp = [sb(f"xp{t}", [128, KCH * NT[t]]) for t in range(TILES)]
        wt = sb("wt", [128, KCH * D])
        braw = sb("braw", [128, D])
        bhi, bmid = sb("bhi", [128, D], bf16), sb("bmid", [128, D], bf16)
        bres1, bres2 = sb("bres1", [128, D]), sb("bres2", [128, D])
        bsum1, bsum2 = sb("bsum1", [128, D]), sb("bsum2", [128, D])
        biases = sb("biases", [128, D], bf16)
        cf = sb("cf", [128, C_FEND])
        chf = sb("chf", [128, H_END])
        ch = sb("ch", [128, H_END], bf16)
        wqkvo = sb("wqkvo", [128, 4 * D])
        wqs = sb("wqs", [128, D])
        wg = sb("wg", [128, E])
        gam, bet = sb("gam", [P, D]), sb("bet", [P, D])
        w1s = sb("w1s", [128, E, F])
        w2s = sb("w2s", [128, E, FCH, D])

        stats = sb("stats", [P, TILES, 3, 6])
        mv = sb("mv", [P, TILES, 3, 2])
        vareps, rstd, power = sb("vareps", [P, TILES, 3]), sb("rstd", [P, TILES, 3]), sb("power", [P, 1])
        hn, hb, hnT = sb("hn", [P, TILES, D]), sb("hb", [P, TILES, D]), sb("hnT", [128, TILES, P])
        qk = sb("qk", [128, TILES, 2 * P])
        v = sb("v", [P, TILES, D])
        nmax, esum, erec = sb("nmax", [P, TILES]), sb("esum", [P, TILES]), sb("erec", [P, TILES])
        prob, attn = sb("prob", [P, TILES, P]), sb("attn", [P, TILES, P])
        attnT, ctxT = sb("attnT", [P, TILES, P]), sb("ctxT", [128, TILES, P])
        o, og, h1 = sb("o", [P, TILES, D]), sb("og", [P, TILES, D]), sb("h1", [P, TILES, D])
        xn, xnT = sb("xn", [P, TILES, D]), sb("xnT", [128, TILES, P])
        gnmax, gexp = sb("gnmax", [P, TILES]), sb("gexp", [P, TILES, E])
        gsum, grec = sb("gsum", [P, TILES]), sb("grec", [P, TILES])
        G = sb("G", [P, TILES, E])
        GT, slotT, slot = sb("GT", [R, P]), sb("slotT", [R, P]), sb("slot", [P, R])
        top8, ninth = sb("top8", [R, TILE_B, 8]), sb("ninth", [R, TILE_B, 8])
        left8, left9, chosen, count = (sb(n, [R, P]) for n in ("left8", "left9", "chosen", "count"))
        pick, wpick = sb("pick", [P, R * SL]), sb("wpick", [P, R * SL])
        exT, hid = sb("exT", [128, E, NS]), sb("hid", [128, EC * NS])
        yT = sb("yT", [128, R * SL])
        y, put = sb("y", [EH * SL, 2 * TILES, D]), sb("put", [EH * SL, 2 * TILES, P])
        res = sb("res", [P, TILES, D])
        warm = sb("warm", [128, BANK], bf16)
        hs = sb("hs", [P, TILES, D])

        bank = [ctx.enter_context(nc.psum_tensor(f"bank{i}", [128, BANK], f32)) for i in range(8)]

        in_x = [sem(f"in_x{t}") for t in range(TILES)]
        in_wt, in_bias, in_cf, in_ch, in_qkvo, in_wg = (sem(n) for n in (
            "in_wt", "in_bias", "in_cf", "in_ch", "in_qkvo", "in_wg"))
        in_gb, in_w1, in_w2, out_done = sem("in_gb"), sem("in_w1"), sem("in_w2"), sem("out_done")
        dve_done = sem("dve_done")
        biases_ready, ch_ready, wqs_ready = sem("biases_ready"), sem("ch_ready"), sem("wqs_ready")
        fills_ready = sem("fills_ready")
        mv_ready = [sem(f"mv_ready{i}") for i in range(3)]
        vareps_ready = [sem(f"vareps_ready{i}") for i in range(3)]
        rstd_ready = [sem(f"rstd_ready{i}") for i in range(3)]
        stats_ready = [sem(f"stats_ready{i}") for i in range(3)]
        power_ready, warm_ready, hs_ready, hb_ready = (sem(n) for n in (
            "power_ready", "warm_ready", "hs_ready", "hb_ready"))
        erec_ready, og_ready, h1_ready = sem("erec_ready"), sem("og_ready"), sem("h1_ready")
        ex_sb_act, yT_sb_act, y_sb_act = sem("ex_sb_act"), sem("yT_sb_act"), sem("y_sb_act")
        h_mm, hn_ready = sem("h_mm"), sem("hn_ready")
        hnT_mm, hnT_sb, qk_mm, qk_sb, v_mm, v_sb = (sem(n) for n in (
            "hnT_mm", "hnT_sb", "qk_mm", "qk_sb", "v_mm", "v_sb"))
        s_mm, nmax_ready, prob_ready, attn_ready = (sem(n) for n in ("s_mm", "nmax_ready", "prob_ready", "attn_ready"))
        attnT_mm, attnT_sb, ctx_mm, ctx_sb = (sem(n) for n in ("attnT_mm", "attnT_sb", "ctx_mm", "ctx_sb"))
        o_mm, o_sb, xn_ready, xnT_mm, xnT_sb = (sem(n) for n in ("o_mm", "o_sb", "xn_ready", "xnT_mm", "xnT_sb"))
        lg_mm, gnmax_ready, gexp_ready = sem("lg_mm"), sem("gnmax_ready"), sem("gexp_ready")
        G_ready, GT_mm, slotT_ready, slot_mm, pick_ready = (sem(n) for n in (
            "G_ready", "GT_mm", "slotT_ready", "slot_mm", "pick_ready"))
        wpick_ready, ex_mm, ex_sb = sem("wpick_ready"), sem("ex_mm"), sem("ex_sb")
        hid_mm, hid_sb, y_mm, yT_sb = sem("hid_mm"), sem("hid_sb"), sem("y_mm"), sem("yT_sb")
        yt_mm, y_sb, put_mm, put_sb = sem("yt_mm"), sem("y_sb"), sem("put_mm"), sem("put_sb")
        res_mm, res_ready = sem("res_mm"), sem("res_ready")

        ident = cf[:, C_ID:C_ID + 128]

        def sel(item, n):
            return ch[:, H_SEL + item:H_SEL + item + 1].broadcast_to([128, n])

        def sel_blocks(item, k, n):
            return ch[:, H_SEL + item:H_SEL + item + k].unsqueeze(2).broadcast_to([128, k, n])

        FULL = sum(n == TILE_B for n in NB)
        SPANS = [(0, FULL, SL)] + [(t, 1, NB[t] * TOPK) for t in range(FULL, TILES)]

        PICK_PARTS = [(2 * p, 2, SL) for p in range(PAIRS - 1)] + [
            (t, 1, NB[t] * TOPK) for t in (TILES - 2, TILES - 1)]

        def slot_cols(buf, t, k, w):
            return buf[:, t * E * SL:t * E * SL + k * E * w].rearrange("p (r w) -> p r w", w=w)

        def half_cols(t, h, w):
            return slice(t * E * SL + h * EH * w, t * E * SL + (h + 1) * EH * w)

        def at(t, stage):
            if 0 <= t < TILES:
                stage(t)

        TOP_BANK, EX_BANK, HID_BANK, Y_BANK = 0, (1, 2, 3), (4, 5, 6, 7, 0, 1), (2, 3, 4)
        PUT_BANK, YT_BANK, RES_BANK = (5, 6, 7), (0, 1, 2), (3, 4, 0)

        def yT_copy(copy, j):
            e0, k = PER_BANK * j, min(PER_BANK, E - PER_BANK * j)
            src = bank[Y_BANK[j]][:, 0:k * NS].rearrange("p (e n) -> p e n", e=k)
            for t, m, w in SPANS:
                dst = yT[:, t * E * SL:t * E * SL + m * E * w].rearrange("p (t e w) -> p t e w", t=m, e=E)
                last = copy(dst[:, :, e0:e0 + k, :].rearrange("p t e w -> p e t w"),
                            src[:, :, t * SL:t * SL + m * w].rearrange("p e (t w) -> p e t w", t=m))
            return last

        block = ctx.enter_context(nc.Block())

        @block.sync
        def _(sp):
            sp.dma_start(braw[:, :], bias_rows).then_inc(in_bias, 16)
            sp.dma_start(wt[:, :], w_tok).then_inc(in_wt, 16)
            sp.dma_start(xp[0][:, :], patches[:, 0:KCH * NT[0]]).then_inc(in_x[0], 16)
            sp.dma_start(cf[:, :], const_f).then_inc(in_cf, 16)
            sp.dma_start(wqkvo[:, :], w_qkvo).then_inc(in_qkvo, 16)
            for t in range(1, TILES):
                at = KCH * sum(NT[:t])
                sp.dma_start(xp[t][:, :], patches[:, at:at + KCH * NT[t]]).then_inc(in_x[t], 16)
            sp.dma_start(w1s[:, :, :], w1).then_inc(in_w1, 16)
            sp.dma_start(w2s[:, :, :, :], w2).then_inc(in_w2, 16)
            for p in range(PAIRS):
                at_row = sum(NT[:2 * p])
                sp.wait_ge(res_ready, 2 * (p + 1) if p < PAIRS - 1 else TILES - 1)
                if p < PAIRS - 1:
                    sp.dma_start(out[at_row:at_row + 2 * P, :].rearrange("(t p) d -> p t d", t=2),
                                 res[:, 2 * p:2 * p + 2, :]).then_inc(out_done, 16)
                else:
                    sp.dma_start(out[at_row:at_row + P, :], res[:, TILES - 2, :]).then_inc(out_done, 16)
            sp.wait_ge(res_ready, TILES)
            sp.dma_start(out[B * S - NT[-1]:B * S, :], res[0:NT[-1], TILES - 1, :]).then_inc(out_done, 16)
            sp.wait_ge(out_done, 16 * (PAIRS + 1))

        @block.gpsimd
        def _(pool):
            nc.gpsimd.memset(gexp[:, :, :], 0.0).then_inc(fills_ready, 1)
            nc.gpsimd.memset(gsum[:, :], 1.0).then_inc(fills_ready, 1)
            nc.gpsimd.memset(ninth[:, :, :], -1.0).then_inc(fills_ready, 1)
            nc.gpsimd.memset(power[:, :], -0.5).then_inc(power_ready, 1)
            pool.wait_ge(power_ready, 1)

            def inv_std(t, which, eps):
                pool.wait_ge(mv_ready[which], t + 1)
                nc.gpsimd.tensor_scalar(vareps[0:NT[t], t, which:which + 1], mv[0:NT[t], t, which, 1:2],
                                        eps, None, ALU.add).then_inc(vareps_ready[which], 1)
                pool.wait_ge(vareps_ready[which], t + 1)
                nc.gpsimd.tensor_tensor(rstd[0:NT[t], t, which:which + 1], vareps[0:NT[t], t, which:which + 1],
                                        power[0:NT[t], :], ALU.pow).then_inc(rstd_ready[which], 1)

            def inv_std_pre(t):
                inv_std(t, 0, EPS_PRE)

            def inv_std_attn(t):
                inv_std(t, 1, EPS_ATTN)

            def inv_std_ffn(t):
                inv_std(t, 2, EPS_PRE)

            def residual_beta(t):
                pool.wait_ge(hs_ready, t + 1)
                if t == 0:
                    pool.wait_ge(in_gb, 32)
                nc.gpsimd.tensor_tensor(hb[0:NT[t], t, :], hs[0:NT[t], t, :], bet[0:NT[t], :],
                                        ALU.add).then_inc(hb_ready, 1)

            for step in range(TILES + 3):
                at(step - 3, inv_std_attn)
                at(step, inv_std_pre)
                at(step - 1, residual_beta)
                at(step - 3, inv_std_ffn)

            for t, k, w in PICK_PARTS:
                pool.wait_ge(pick_ready, t // 2 + 1)
                last = nc.gpsimd.tensor_tensor(
                    slot_cols(wpick, t, k, w), slot_cols(pick, t, k, w),
                    G[:, t:t + k, :].rearrange("p t e -> p (t e)").unsqueeze(2).broadcast_to([P, k * E, w]),
                    ALU.mult)
            last.then_inc(wpick_ready, 1)

        @block.scalar
        def _(act):
            act.dma_start(chf[:, :], const_h).then_inc(in_ch, 16)
            act.dma_start(gam[:, :], gamma.partition_broadcast(P)).then_inc(in_gb, 16)
            act.dma_start(bet[:, :], beta.partition_broadcast(P)).then_inc(in_gb, 16)
            act.dma_start(wg[:, :], w_gate).then_inc(in_wg, 16)

            def hnT_copy(t):
                act.wait_ge(hnT_mm, t + 1)
                nc.scalar.activation(hnT[:, t, 0:NT[t]], bank[2][:, 0:NT[t]], ACT.Copy).then_inc(hnT_sb, 1)

            def v_relu(t):
                act.wait_ge(v_mm, t + 1)
                nc.scalar.activation(v[0:NT[t], t, :], bank[2][0:NT[t], 128:256], ACT.Relu).then_inc(v_sb, 1)

            def qk_relu(t):
                act.wait_ge(qk_mm, t + 1)
                nc.scalar.activation(qk[:, t, 0:2 * NT[t]], bank[3][:, 0:2 * NT[t]], ACT.Relu).then_inc(qk_sb, 1)

            def h_copy(t):
                act.wait_ge(hn_ready, t + 1)
                nc.scalar.activation(hs[0:NT[t], t, :], bank[t % 2][0:NT[t], 0:D], ACT.Copy).then_inc(hs_ready, 1)

            def softmax_exp(t):
                act.wait_ge(nmax_ready, t + 1)
                nc.scalar.activation(prob[0:NT[t], t, 0:NT[t]], bank[4][0:NT[t], 0:NT[t]], ACT.Exp,
                                     bias=nmax[0:NT[t], t:t + 1],
                                     accum_out=esum[0:NT[t], t:t + 1]).then_inc(prob_ready, 1)

            def attnT_copy(t):
                act.wait_ge(attnT_mm, t + 1)
                nc.scalar.activation(attnT[0:NT[t], t, 0:NT[t]], bank[5][0:NT[t], 0:NT[t]],
                                     ACT.Copy).then_inc(attnT_sb, 1)

            def ctx_copy(t):
                act.wait_ge(ctx_mm, t + 1)
                nc.scalar.activation(ctxT[:, t, 0:NT[t]], bank[5][:, 128:128 + NT[t]], ACT.Copy).then_inc(ctx_sb, 1)

            def o_relu(t):
                act.wait_ge(o_mm, t + 1)
                nc.scalar.activation(o[0:NT[t], t, :], bank[6][0:NT[t], 0:D], ACT.Relu).then_inc(o_sb, 1)

            def xnT_copy(t):
                act.wait_ge(xnT_mm, t + 1)
                nc.scalar.activation(xnT[:, t, 0:NT[t]], bank[7][:, 128:128 + NT[t]], ACT.Copy).then_inc(xnT_sb, 1)

            def gate_exp(t):
                act.wait_ge(gnmax_ready, t + 1)
                if t == 0:
                    act.wait_ge(fills_ready, 2)
                nc.scalar.activation(gexp[0:NT[t], t, :], bank[7][0:NT[t], E * t:E * t + E], ACT.Exp,
                                     bias=gnmax[0:NT[t], t:t + 1],
                                     accum_out=gsum[0:NT[t], t:t + 1]).then_inc(gexp_ready, 1)

            for step in range(TILES + 5):
                at(step - 2, softmax_exp)
                at(step - 3, o_relu)
                at(step - 1, hnT_copy)
                at(step - 1, h_copy)
                at(step - 5, gate_exp)
                at(step - 1, qk_relu)
                at(step - 2, attnT_copy)
                at(step - 1, v_relu)
                at(step - 4, xnT_copy)
                at(step - 2, ctx_copy)

            act.wait_ge(ex_mm, 2)
            nc.scalar.activation(exT[:, :, 2 * SL:4 * SL].rearrange("p e (t w) -> p t e w", t=2),
                                 bank[EX_BANK[1]][:, 0:2 * E * SL].rearrange("p (t e w) -> p t e w", t=2, e=E),
                                 ACT.Copy).then_inc(ex_sb_act, 1)
            for k in range(HID_BANKS):
                n = min(PER_BANK, EC - PER_BANK * k) * NS
                act.wait_ge(hid_mm, k + 1)
                nc.scalar.activation(hid[:, k * PER_BANK * NS:k * PER_BANK * NS + n], bank[HID_BANK[k]][:, 0:n],
                                     ACT.Gelu).then_inc(hid_sb, 1)
            act.wait_ge(y_mm, 2)
            yT_copy(nc.scalar.copy, 1).then_inc(yT_sb_act, 1)
            act.wait_ge(yt_mm, 2)
            nc.scalar.activation(y[:, 4:8, :].rearrange("p b d -> p (b d)"), bank[YT_BANK[1]][0:EH * SL, :],
                                 ACT.Copy).then_inc(y_sb_act, 1)

        @block.vector
        def _(dve):
            done = [0]

            def chain(ins):
                done[0] += 1
                ins.then_inc(dve_done, 1)
                dve.wait_ge(dve_done, done[0])

            def stats_of(src, t, which):
                nc.vector.bn_stats(stats[0:NT[t], t, which, :], src).then_inc(stats_ready[which], 1)

            def mean_var(t, which):
                dve.wait_ge(stats_ready[which], t + 1)
                nc.vector.bn_aggr(mv[0:NT[t], t, which, :], stats[0:NT[t], t, which, :]).then_inc(mv_ready[which], 1)

            def normalise(dst, src, t, which):
                dve.wait_ge(mv_ready[which], t + 1)
                dve.wait_ge(rstd_ready[which], t + 1)
                return nc.vector.tensor_scalar(dst, src, mv[0:NT[t], t, which, 0:1],
                                               rstd[0:NT[t], t, which:which + 1], ALU.subtract, ALU.mult)

            nc.vector.memset(warm[:, :], 0.0).then_inc(warm_ready, 1)
            dve.wait_ge(in_bias, 16)
            chain(nc.vector.tensor_copy(bhi[:, :], braw[:, :]))
            chain(nc.vector.tensor_tensor(bres1[:, :], braw[:, :], bhi[:, :], ALU.subtract))
            chain(nc.vector.tensor_copy(bmid[:, :], bres1[:, :]))
            chain(nc.vector.tensor_tensor(bres2[:, :], bres1[:, :], bmid[:, :], ALU.subtract))
            dve.wait_ge(in_ch, 16)
            nc.vector.tensor_copy(ch[:, :], chf[:, :]).then_inc(ch_ready, 1)
            dve.wait_ge(in_cf, 16)
            chain(nc.vector.tensor_scalar(bsum1[:, :], bhi[:, :], cf[:, C_PART:C_PART + 1], None, ALU.mult))
            chain(nc.vector.scalar_tensor_tensor(bsum2[:, :], bmid[:, :], cf[:, C_PART + 1:C_PART + 2],
                                                 bsum1[:, :], ALU.mult, ALU.add))
            nc.vector.scalar_tensor_tensor(biases[:, :], bres2[:, :], cf[:, C_PART + 2:C_PART + 3],
                                           bsum2[:, :], ALU.mult, ALU.add).then_inc(biases_ready, 1)
            dve.wait_ge(in_qkvo, 16)
            nc.vector.tensor_scalar(wqs[:, :], wqkvo[:, 0:D], SCALE, None, ALU.mult).then_inc(wqs_ready, 1)

            def h_stats(t):
                dve.wait_ge(h_mm, t + 1)
                stats_of(bank[t % 2][0:NT[t], 0:D], t, 0)

            def h_mean_var(t):
                mean_var(t, 0)

            def pre_norm(t):
                normalise(hn[0:NT[t], t, :], bank[t % 2][0:NT[t], 0:D], t, 0).then_inc(hn_ready, 1)

            def row_max(t):
                dve.wait_ge(s_mm, t + 1)
                nc.vector.tensor_reduce(nmax[0:NT[t], t:t + 1], bank[4][0:NT[t], 0:NT[t]], AX.X, ALU.max,
                                        negate=True).then_inc(nmax_ready, 1)

            def row_recip(t):
                dve.wait_ge(prob_ready, t + 1)
                nc.vector.reciprocal(erec[0:NT[t], t:t + 1], esum[0:NT[t], t:t + 1]).then_inc(erec_ready, 1)

            def attn_norm(t):
                dve.wait_ge(erec_ready, t + 1)
                nc.vector.tensor_scalar(attn[0:NT[t], t, 0:NT[t]], prob[0:NT[t], t, 0:NT[t]],
                                        erec[0:NT[t], t:t + 1], None, ALU.mult).then_inc(attn_ready, 1)

            def o_stats(t):
                dve.wait_ge(o_sb, t + 1)
                stats_of(o[0:NT[t], t, :], t, 1)

            def o_mean_var(t):
                mean_var(t, 1)

            def o_gamma(t):
                dve.wait_ge(mv_ready[1], t + 1)
                if t == 0:
                    dve.wait_ge(in_gb, 32)
                nc.vector.scalar_tensor_tensor(og[0:NT[t], t, :], o[0:NT[t], t, :], mv[0:NT[t], t, 1, 0:1],
                                               gam[0:NT[t], :], ALU.subtract, ALU.mult).then_inc(og_ready, 1)

            def o_residual(t):
                dve.wait_ge(og_ready, t + 1)
                dve.wait_ge(rstd_ready[1], t + 1)
                dve.wait_ge(hb_ready, t + 1)
                nc.vector.scalar_tensor_tensor(h1[0:NT[t], t, :], og[0:NT[t], t, :], rstd[0:NT[t], t, 1:2],
                                               hb[0:NT[t], t, :], ALU.mult, ALU.add).then_inc(h1_ready, 1)

            def h1_stats(t):
                dve.wait_ge(h1_ready, t + 1)
                stats_of(h1[0:NT[t], t, :], t, 2)

            def h1_mean_var(t):
                mean_var(t, 2)

            def ffn_norm(t):
                normalise(xn[0:NT[t], t, :], h1[0:NT[t], t, :], t, 2).then_inc(xn_ready, 1)

            def gate_max(t):
                dve.wait_ge(lg_mm, t + 1)
                nc.vector.tensor_reduce(gnmax[0:NT[t], t:t + 1], bank[7][0:NT[t], E * t:E * t + E], AX.X, ALU.max,
                                        negate=True).then_inc(gnmax_ready, 1)

            for step in range(TILES + 5):
                at(step - 2, row_max)
                at(step - 4, h1_stats)
                at(step - 1, pre_norm)
                at(step - 4, h1_mean_var)
                at(step - 2, row_recip)
                at(step - 2, attn_norm)
                at(step - 3, o_stats)
                at(step - 5, gate_max)
                at(step - 3, o_mean_var)
                at(step - 4, ffn_norm)
                at(step, h_stats)
                at(step, h_mean_var)
                at(step - 3, o_gamma)
                at(step - 3, o_residual)

            dve.wait_ge(gexp_ready, TILES)
            chain(nc.vector.reciprocal(grec[:, :], gsum[:, :]))
            nc.vector.tensor_tensor(G[:, :, :], gexp[:, :, :], grec[:, :].unsqueeze(2).broadcast_to([P, TILES, E]),
                                    ALU.mult).then_inc(G_ready, 1)

            dve.wait_ge(GT_mm, 1)
            chain(nc.vector.tensor_copy(GT[:, :], bank[TOP_BANK][0:R, 0:P]))
            for b in range(TILE_B):
                last = nc.vector.max(top8[:, b, :], GT[:, b * S:(b + 1) * S])
            chain(last)
            for b in range(TILE_B):
                last = nc.vector.match_replace(left8[:, b * S:(b + 1) * S], top8[:, b, :],
                                               GT[:, b * S:(b + 1) * S], -1.0)
            chain(last)
            dve.wait_ge(fills_ready, 3)
            chain(nc.vector.tensor_reduce(ninth[:, :, 0], left8[:, :].rearrange("r (b s) -> r b s", b=TILE_B),
                                          AX.X, ALU.max))
            for b in range(TILE_B):
                last = nc.vector.match_replace(left9[:, b * S:(b + 1) * S], ninth[:, b, :],
                                               left8[:, b * S:(b + 1) * S], -1.0)
            chain(last)
            chain(nc.vector.tensor_scalar(chosen[:, :], left9[:, :], 0.0, None, ALU.is_lt))
            chain(nc.vector.tensor_tensor_scan(count[:, :], chosen[:, :], chosen[:, :], 0.0, ALU.add, ALU.max))
            nc.vector.tensor_tensor(slotT[:, :], count[:, :], chosen[:, :], ALU.mult).then_inc(slotT_ready, 1)

            dve.wait_ge(slot_mm, 1)
            chain(nc.vector.tensor_copy(slot[:, :], bank[TOP_BANK][0:P, 128:128 + R]))
            for t, k, w in PICK_PARTS:
                last = nc.vector.tensor_tensor(
                    slot_cols(pick, t, k, w), slot[:, E * t:E * (t + k)].unsqueeze(2).broadcast_to([P, k * E, w]),
                    cf[0:P, C_IOTA:C_IOTA + w].unsqueeze(1).broadcast_to([P, k * E, w]), ALU.is_equal)
                if t != 4:
                    last.then_inc(pick_ready, 1)

            dve.wait_ge(ex_mm, 1)
            nc.vector.tensor_copy(exT[:, :, 0:2 * SL].rearrange("p e (t w) -> p t e w", t=2),
                                  bank[EX_BANK[0]][:, 0:2 * E * SL].rearrange("p (t e w) -> p t e w", t=2, e=E)
                                  ).then_inc(ex_sb, 1)
            dve.wait_ge(ex_mm, 3)
            for i, t in enumerate((4, 5)):
                n = NB[t] * TOPK
                last = nc.vector.tensor_copy(
                    exT[:, :, t * SL:t * SL + n],
                    bank[EX_BANK[2]][:, i * E * SL:i * E * SL + E * n].rearrange("p (e n) -> p e n", e=E))
            last.then_inc(ex_sb, 1)

            for p in range(PAIRS):
                dve.wait_ge(put_mm, p + 1)
                for t in (2 * p, 2 * p + 1):
                    w, n = EH * NB[t] * TOPK, NT[t]
                    src = bank[PUT_BANK[p]][0:w, (t % 2) * 2 * P:(t % 2) * 2 * P + 2 * P]
                    last = nc.vector.tensor_copy(put[0:w, 2 * t:2 * t + 2, 0:n],
                                                 src.rearrange("w (h n) -> w h n", h=2)[:, :, 0:n])
                last.then_inc(put_sb, 1)

            for j in (0, 2):
                dve.wait_ge(y_mm, j + 1)
                yT_copy(nc.vector.tensor_copy, j).then_inc(yT_sb, 1)

            dve.wait_ge(yt_mm, 1)
            nc.vector.tensor_copy(y[:, 0:4, :].rearrange("p b d -> p (b d)"),
                                  bank[YT_BANK[0]][0:EH * SL, :]).then_inc(y_sb, 1)
            dve.wait_ge(yt_mm, 3)
            for t in (4, 5):
                w = EH * NB[t] * TOPK
                last = nc.vector.tensor_copy(y[0:w, 2 * t:2 * t + 2, :].rearrange("p b d -> p (b d)"),
                                             bank[YT_BANK[2]][0:w, (t % 2) * 2 * D:(t % 2 + 1) * 2 * D])
            last.then_inc(y_sb, 1)

            for p in range(PAIRS):
                dve.wait_ge(res_mm, p + 1)
                if p < PAIRS - 1:
                    nc.vector.tensor_tensor(res[:, 2 * p:2 * p + 2, :].rearrange("p t d -> p (t d)"),
                                            bank[RES_BANK[p]][0:P, 0:2 * D],
                                            h1[:, 2 * p:2 * p + 2, :].rearrange("p t d -> p (t d)"),
                                            ALU.add).then_inc(res_ready, 2)
                else:
                    for t in (2 * p, 2 * p + 1):
                        nc.vector.tensor_tensor(res[0:NT[t], t, :],
                                                bank[RES_BANK[p]][0:NT[t], (t % 2) * D:(t % 2 + 1) * D],
                                                h1[0:NT[t], t, :], ALU.add).then_inc(res_ready, 1)

        @block.tensor
        def _(pe):
            def embed(t, part):
                h = bank[t % 2][0:NT[t], 0:D]
                n = NT[t]
                if part == 0:
                    pe.wait_ge(in_x[t], 16)
                    if t == 0:
                        pe.wait_ge(in_wt, 16)
                    if t >= 2:
                        pe.wait_ge(hs_ready, t - 1)
                for c in range(2 * part, 2 * part + 2):
                    nc.tensor.matmul(h, xp[t][:, c * n:(c + 1) * n], wt[:, c * D:(c + 1) * D],
                                     start=(c == 0), stop=False)
                if part == 2:
                    if t == 0:
                        pe.wait_ge(ch_ready, 1)
                        pe.wait_ge(biases_ready, 1)
                    nc.tensor.matmul(h, ch[:, H_TOK:H_TOK + n], biases[:, :], start=False,
                                     stop=True).then_inc(h_mm, 1)

            def hn_transpose(t):
                pe.wait_ge(hn_ready, t + 1)
                if t == 0:
                    pe.wait_ge(in_cf, 16)
                if t >= 1:
                    pe.wait_ge(v_sb, t)
                nc.tensor.transpose(bank[2][:, 0:NT[t]], hn[0:NT[t], t, :], ident[0:NT[t], 0:NT[t]]).then_inc(hnT_mm, 1)

            def queries_keys(t):
                n = NT[t]
                pe.wait_ge(hnT_sb, t + 1)
                if t == 0:
                    pe.wait_ge(in_qkvo, 16)
                    pe.wait_ge(wqs_ready, 1)
                if t >= 1:
                    pe.wait_ge(qk_sb, t)
                nc.tensor.matmul(bank[3][:, 0:n], wqs[:, :], hnT[:, t, 0:n], start=True, stop=False)
                nc.tensor.matmul(bank[3][:, 0:n], biases[:, :], sel(I_Q, n), start=False, stop=True)
                nc.tensor.matmul(bank[3][:, n:2 * n], wqkvo[:, D:2 * D], hnT[:, t, 0:n], start=True, stop=False)
                nc.tensor.matmul(bank[3][:, n:2 * n], biases[:, :], sel(I_K, n), start=False,
                                 stop=True).then_inc(qk_mm, 1)

            def values(t):
                n = NT[t]
                nc.tensor.matmul(bank[2][0:n, 128:256], hnT[:, t, 0:n], wqkvo[:, 2 * D:3 * D], start=True, stop=False)
                nc.tensor.matmul(bank[2][0:n, 128:256], sel(I_V, n), biases[:, :], start=False,
                                 stop=True).then_inc(v_mm, 1)

            def scores(t):
                n = NT[t]
                pe.wait_ge(qk_sb, t + 1)
                if t >= 1:
                    pe.wait_ge(prob_ready, t)
                s = bank[4][0:n, 0:n]
                nc.tensor.matmul(s, ch[:, H_ML:H_ML + n], ch[:, H_MR:H_MR + n], start=True, stop=False)
                nc.tensor.matmul(s, qk[:, t, 0:n], qk[:, t, n:2 * n], start=False, stop=True).then_inc(s_mm, 1)

            def attn_transpose(t):
                n = NT[t]
                pe.wait_ge(attn_ready, t + 1)
                if t >= 1:
                    pe.wait_ge(ctx_sb, t)
                nc.tensor.transpose(bank[5][0:n, 0:n], attn[0:n, t, 0:n], ident[0:n, 0:n]).then_inc(attnT_mm, 1)

            def context(t):
                n = NT[t]
                pe.wait_ge(attnT_sb, t + 1)
                pe.wait_ge(v_sb, t + 1)
                nc.tensor.matmul(bank[5][:, 128:128 + n], v[0:n, t, :], attnT[0:n, t, 0:n], start=True,
                                 stop=True).then_inc(ctx_mm, 1)

            def project(t):
                n = NT[t]
                pe.wait_ge(ctx_sb, t + 1)
                if t >= 1:
                    pe.wait_ge(o_sb, t)
                nc.tensor.matmul(bank[6][0:n, 0:D], ctxT[:, t, 0:n], wqkvo[:, 3 * D:4 * D], start=True, stop=False)
                nc.tensor.matmul(bank[6][0:n, 0:D], sel(I_O, n), biases[:, :], start=False,
                                 stop=True).then_inc(o_mm, 1)

            def xn_transpose(t):
                pe.wait_ge(xn_ready, t + 1)
                if t >= 1:
                    pe.wait_ge(gexp_ready, t)
                nc.tensor.transpose(bank[7][:, 128:128 + NT[t]], xn[0:NT[t], t, :],
                                    ident[0:NT[t], 0:NT[t]]).then_inc(xnT_mm, 1)

            def gate(t):
                pe.wait_ge(xnT_sb, t + 1)
                if t == 0:
                    pe.wait_ge(in_wg, 16)
                nc.tensor.matmul(bank[7][0:NT[t], E * t:E * t + E], xnT[:, t, 0:NT[t]], wg[:, :], start=True,
                                 stop=True).then_inc(lg_mm, 1)

            def embed_a(t):
                embed(t, 0)

            def embed_b(t):
                embed(t, 1)

            def embed_c(t):
                embed(t, 2)

            def fill(count):
                for _ in range(count):
                    nc.tensor.matmul(bank[7][:, :], warm[:, 0:128], warm[:, :], start=True, stop=True)

            pe.wait_ge(warm_ready, 1)
            fill(WARM_START)
            for step in range(TILES + 5):
                at(step, embed_a)
                at(step - 3, project)
                at(step, embed_b)
                at(step - 1, hn_transpose)
                at(step - 5, gate)
                at(step, embed_c)
                at(step - 1, queries_keys)
                at(step - 2, attn_transpose)
                at(step - 1, values)
                at(step - 4, xn_transpose)
                at(step - 1, scores)
                at(step - 2, context)

            pe.wait_ge(G_ready, 1)
            nc.tensor.transpose(bank[TOP_BANK][0:R, 0:P], G[:, :, :].rearrange("p t e -> p (t e)"),
                                ident[0:P, 0:P]).then_inc(GT_mm, 1)
            fill(WARM_TOPK)
            pe.wait_ge(slotT_ready, 1)
            nc.tensor.transpose(bank[TOP_BANK][0:P, 128:128 + R], slotT[:, :], ident[0:R, 0:R]).then_inc(slot_mm, 1)

            for p in range(PAIRS):
                pe.wait_ge(pick_ready, p + 1)
                for t in (2 * p, 2 * p + 1):
                    n = NB[t] * TOPK
                    at_col = (t % 2) * E * SL
                    last = nc.tensor.matmul(bank[EX_BANK[p]][:, at_col:at_col + E * n], xn[0:NT[t], t, :],
                                            pick[0:NT[t], t * E * SL:t * E * SL + E * n], start=True, stop=True)
                last.then_inc(ex_mm, 1)

            pe.wait_ge(in_w1, 16)
            pe.wait_ge(ex_sb, 2)
            pe.wait_ge(ex_sb_act, 1)
            for k in range(HID_BANKS):
                k0, kn = PER_BANK * k, min(PER_BANK, EC - PER_BANK * k)
                hb_ = bank[HID_BANK[k]]
                nc.tensor.matmul(hb_[:, 0:kn * NS], biases[:, :], sel_blocks(I_B1 + k0, kn, NS),
                                 start=True, stop=False, skip_group_check=True)
                for ec in range(k0, k0 + kn):
                    e, c = ec // FCH, ec % FCH
                    last = nc.tensor.matmul(hb_[:, (ec - k0) * NS:(ec - k0 + 1) * NS],
                                            w1s[:, e, c * 128:(c + 1) * 128], exT[:, e, :], start=False,
                                            stop=ec == k0 + kn - 1, skip_group_check=True)
                last.then_inc(hid_mm, 1)

            pe.wait_ge(wpick_ready, 1)
            for p in range(PAIRS):
                pe.wait_ge(hid_sb, HID_BANK.index(PUT_BANK[p]) + 1)
                for t in (2 * p, 2 * p + 1):
                    n, w = NT[t], NB[t] * TOPK
                    for h in range(2):
                        at_col = ((t % 2) * 2 + h) * P
                        last = nc.tensor.transpose(bank[PUT_BANK[p]][0:EH * w, at_col:at_col + n],
                                                   wpick[0:n, half_cols(t, h, w)], ident[0:n, 0:n])
                last.then_inc(put_mm, 1)

            pe.wait_ge(in_w2, 16)
            for j in range(Y_BANKS):
                e0, k = PER_BANK * j, min(PER_BANK, E - PER_BANK * j)
                nc.tensor.matmul(bank[Y_BANK[j]][:, 0:k * NS], biases[:, :], sel_blocks(I_B2 + e0, k, NS),
                                 start=True, stop=False, skip_group_check=True)
                for e in range(e0, e0 + k):
                    for c in range(FCH):
                        ec = FCH * e + c
                        pe.wait_ge(hid_sb, ec // PER_BANK + 1)
                        last = nc.tensor.matmul(bank[Y_BANK[j]][:, (e - e0) * NS:(e - e0 + 1) * NS],
                                                w2s[:, e, c, :], hid[:, ec * NS:(ec + 1) * NS], start=False,
                                                stop=(e == e0 + k - 1 and c == FCH - 1), skip_group_check=True)
                last.then_inc(y_mm, 1)

            pe.wait_ge(hid_sb, HID_BANKS)
            pe.wait_ge(yT_sb, 2)
            pe.wait_ge(yT_sb_act, 1)
            for p in range(PAIRS):
                for t in (2 * p, 2 * p + 1):
                    w = NB[t] * TOPK
                    for h in range(2):
                        at_col = ((t % 2) * 2 + h) * D
                        last = nc.tensor.transpose(bank[YT_BANK[p]][0:EH * w, at_col:at_col + D],
                                                   yT[:, half_cols(t, h, w)], ident[:, :])
                last.then_inc(yt_mm, 1)

            for p in range(PAIRS):
                pe.wait_ge(put_sb, p + 1)
                if p == 1:
                    pe.wait_ge(y_sb_act, 1)
                else:
                    pe.wait_ge(y_sb, 1 + p // 2)
                for t in (2 * p, 2 * p + 1):
                    w = EH * NB[t] * TOPK
                    for h in range(2):
                        last = nc.tensor.matmul(bank[RES_BANK[p]][0:NT[t], (t % 2) * D:(t % 2 + 1) * D],
                                                put[0:w, 2 * t + h, 0:NT[t]], y[0:w, 2 * t + h, :],
                                                start=h == 0, stop=h == 1)
                last.then_inc(res_mm, 1)


def kernel(x, cls_tok, L0_tok_w, L0_tok_b, L0_attn_Wq, L0_attn_bq, L0_attn_Wk, L0_attn_bk, L0_attn_Wv, L0_attn_bv,
           L0_attn_Wo, L0_attn_bo, L0_attn_gamma, L0_attn_beta, L0_ffn_Wg, L0_ffn_W1, L0_ffn_b1, L0_ffn_W2, L0_ffn_b2):
    import concourse.bacc as bacc
    from concourse.bass_utils import run_bass_kernel_spmd

    px = np.asarray(x).reshape(B, C, HP, PATCH, HP, PATCH).transpose(1, 3, 5, 0, 2, 4).reshape(KCH, 128, B, S - 1)
    full = np.zeros((KCH, 128, B, S), np.float32)
    full[:, :, :, 1:] = px
    full = full.transpose(1, 0, 2, 3)
    patches = np.concatenate([full[:, :, TILE_B * t:TILE_B * t + NB[t]].reshape(128, KCH * NT[t])
                              for t in range(TILES)], axis=1)
    w_tok = np.asarray(L0_tok_w).reshape(D, KCH, 128).transpose(2, 1, 0).reshape(128, KCH * D)
    rows = np.concatenate([np.asarray(a).reshape(-1, D) for a in (
        L0_tok_b, cls_tok, L0_attn_bq, L0_attn_bk, L0_attn_bv, L0_attn_bo, L0_ffn_b1, L0_ffn_b2)])
    bias_rows = np.zeros((128, D), np.float32)
    bias_rows[0:3 * ITEMS] = np.repeat(rows, 3, axis=0)
    const_f, const_h = constants()
    w_qkvo = np.concatenate([np.asarray(a) for a in (L0_attn_Wq, L0_attn_Wk, L0_attn_Wv, L0_attn_Wo)], axis=1)
    arrays = {
        "patches": patches, "w_tok": w_tok, "bias_rows": bias_rows, "const_f": const_f, "const_h": const_h,
        "w_qkvo": w_qkvo, "w_gate": np.asarray(L0_ffn_Wg), "gamma": np.asarray(L0_attn_gamma),
        "beta": np.asarray(L0_attn_beta), "w1": np.asarray(L0_ffn_W1).transpose(1, 0, 2),
        "w2": np.asarray(L0_ffn_W2).reshape(E, FCH, 128, D).transpose(2, 0, 1, 3),
    }
    arrays = {name: np.ascontiguousarray(a) for name, a in arrays.items()}
    nc = bacc.Bacc("TRN2", target_bir_lowering=False, num_devices=1)
    args = [nc.dram_tensor(name, a.shape, mybir.dt.float32, kind="ExternalInput").ap() for name, a in arrays.items()]
    out = nc.dram_tensor("out", (B * S, D), mybir.dt.float32, kind="ExternalOutput").ap()
    vit_block(nc, *args, out)
    r = run_bass_kernel_spmd(nc, [arrays], core_ids=[0])
    return r.results[0]["out"].reshape(B, S, D)
```

```python
import numpy as np
import concourse.bass as bass
from concourse import mybir
from contextlib import ExitStack

B, C, IMG, PATCH, D = 16, 3, 96, 16, 128
HP = IMG // PATCH
S = HP * HP + 1
KCH = C * PATCH * PATCH // 128
E, F = 8, 256
FCH = F // 128
TOPK = min(max(int(S * 2 / E), 1), S)
SCALE = 16 ** -0.5
EPS_PRE, EPS_ATTN = 1e-5, 1e-3

TILE_B = 3
TILES = -(-B // TILE_B)
NB = [min(TILE_B, B - TILE_B * t) for t in range(TILES)]
NT = [n * S for n in NB]
P = TILE_B * S
SL = TILE_B * TOPK
RT = B * E
R = TILES * E
NS = B * TOPK
EH = E // 2
BANK = 512
EC = E * FCH
PER_BANK = BANK // NS
HID_BANKS = -(-EC // PER_BANK)
Y_BANKS = -(-E // PER_BANK)
PAIRS = TILES // 2
WARM_START, WARM_GATE, WARM_TOPK, WARM_PICK = 6, 1, 6, 2
MASK_OFF = -2.0 ** 100

I_TOK, I_CLS, I_O = range(3)
ITEMS = I_O + 1
BR = 3 * ITEMS
X_Q, X_K, X_V, X_B1, X_B2, X_END = 0, 1, 2, 3, 3 + EC, 3 + EC + E

C_ID, C_SLOT, C_POS, C_IMG, C_FEND = np.cumsum([0, 128, EH * SL, S, TILE_B]).tolist()
H_SEL, H_TOK, H_ML, H_MR, H_END = 0, ITEMS, ITEMS + P, ITEMS + 2 * P, ITEMS + 3 * P


def constants():
    cf = np.zeros((128, C_FEND), np.float32)
    cf[:, C_ID:C_ID + 128] = np.eye(128)
    n = np.arange(P)
    for b in range(TILE_B):
        for e in range(EH):
            c0 = C_SLOT + e * SL + b * TOPK
            cf[0:P, c0:c0 + TOPK] = np.where((n // S == b)[:, None], np.arange(1, TOPK + 1), -1)
        cf[0:P, C_IMG + b] = n // S == b
    cf[0:P, C_POS:C_POS + S] = (n % S)[:, None] == np.arange(S)
    ch = np.zeros((BR, H_END), np.float32)
    for p in range(BR):
        ch[p, H_SEL + p // 3] = 1.0
    for s in range(3):
        ch[3 * I_TOK + s, H_TOK:H_TOK + P] = n % S != 0
        ch[3 * I_CLS + s, H_TOK:H_TOK + P] = n % S == 0
    for b in range(TILE_B):
        ch[b, H_ML:H_ML + P] = n // S == b
        ch[b, H_MR:H_MR + P] = np.where(n // S == b, 0.0, MASK_OFF)
    part = np.zeros((BR, 3), np.float32)
    for p in range(BR):
        part[p, p % 3] = 1.0
    return cf, ch, part


def vit_block(nc, patches, w_tok, bias_rows, feature_biases, const_f, const_h, w_qkvo, w_gate, gamma, beta,
              w1, w2, out):
    f32, bf16 = mybir.dt.float32, mybir.dt.bfloat16
    ALU, ACT, AX = mybir.AluOpType, mybir.ActivationFunctionType, mybir.AxisListType

    ctx = ExitStack()
    with ctx:
        def sb(name, shape, dt=f32):
            return ctx.enter_context(nc.sbuf_tensor(name, shape, dt))

        def sem(name):
            return ctx.enter_context(nc.semaphore(name))

        xp = [sb(f"xp{t}", [128, KCH * NT[t]]) for t in range(TILES)]
        wt = sb("wt", [128, KCH * D])
        braw = sb("braw", [BR, D + 3])
        bhi, bmid = sb("bhi", [BR, D], bf16), sb("bmid", [BR, D], bf16)
        bres1, bres2 = sb("bres1", [BR, D]), sb("bres2", [BR, D])
        bsum1, bsum2 = sb("bsum1", [BR, D]), sb("bsum2", [BR, D])
        biases = sb("biases", [BR, D], bf16)
        xb, bqs = sb("xb", [128, X_END]), sb("bqs", [128, 1])
        cf = sb("cf", [128, C_FEND])
        chf = sb("chf", [BR, H_END])
        ch = sb("ch", [BR, H_END], bf16)
        wqkvo = sb("wqkvo", [128, 4 * D])
        wqs = sb("wqs", [128, D])
        wg = sb("wg", [128, E])
        gam, bet = sb("gam", [P, D]), sb("bet", [P, D])
        w1s = sb("w1s", [128, E, F])
        w2s = sb("w2s", [128, E, FCH, D])

        stats = sb("stats", [P, TILES, 3, 6])
        mv = sb("mv", [P, TILES, 3, 2])
        vareps, rstd, power = sb("vareps", [P, TILES, 3]), sb("rstd", [P, TILES, 3]), sb("power", [P, 1])
        hn, hb, hnT = sb("hn", [P, TILES, D]), sb("hb", [P, TILES, D]), sb("hnT", [128, TILES, P])
        qkv = sb("qkv", [128, TILES, 3 * P])
        vo = sb("vo", [P, TILES, D])
        nmax, esum, erec = sb("nmax", [P, TILES]), sb("esum", [P, TILES]), sb("erec", [P, TILES])
        prob, probT = sb("prob", [P, TILES, P]), sb("probT", [P, TILES, P])
        o, og, h1 = sb("o", [P, TILES, D]), sb("og", [P, TILES, D]), sb("h1", [P, TILES, D])
        xc, xcT = sb("xc", [P, TILES, D]), sb("xcT", [128, TILES, P])
        xn, cmax = sb("xn", [P, TILES, D]), sb("cmax", [P, TILES])
        gnmax, gexp = sb("gnmax", [P, TILES]), sb("gexp", [P, TILES, E])
        gsum, grec = sb("gsum", [P, TILES]), sb("grec", [P, TILES])
        G = sb("G", [P, TILES, E])
        Gimg = sb("Gimg", [P, TILES * RT])
        slotT = sb("slotT", [RT, TILE_B, S], bf16)
        top8, ninth = sb("top8", [RT, 8]), sb("ninth", [RT, 8])
        left8, left9, chosen, count = (sb(n, [RT, S]) for n in ("left8", "left9", "chosen", "count"))
        identb, slotb = sb("identb", [128, 128], bf16), sb("slotb", [P, EH * SL], bf16)
        xpart, xleft = sb("xpart", [P, 3, TILES, D], bf16), sb("xleft", [P, TILES, D])
        pick, wpick = sb("pick", [P, R * SL], bf16), sb("wpick", [P, R * SL])
        exT, hid = sb("exT", [128, E, NS]), sb("hid", [128, EC * NS])
        yT = sb("yT", [128, R * SL])
        y, put = sb("y", [EH * SL, 2 * TILES, D]), sb("put", [EH * SL, 2 * TILES, P])
        res = sb("res", [P, TILES, D])
        warm = sb("warm", [128, BANK], bf16)
        hs = sb("hs", [P, TILES, D])

        bank = [ctx.enter_context(nc.psum_tensor(f"bank{i}", [128, BANK], f32)) for i in range(8)]

        in_x = [sem(f"in_x{t}") for t in range(TILES)]
        in_wt, in_x0 = [sem(f"in_wt{i}") for i in range(2)], [sem(f"in_x0_{i}") for i in range(2)]
        in_bias, in_cf, in_ch, in_qkvo, in_wg = (sem(n) for n in (
            "in_bias", "in_cf", "in_ch", "in_qkvo", "in_wg"))
        in_xb, in_gb, in_w1, in_w2, out_done = sem("in_xb"), sem("in_gb"), sem("in_w1"), sem("in_w2"), sem("out_done")
        dve_done = sem("dve_done")
        biases_ready, ch_ready, wqs_ready = sem("biases_ready"), sem("ch_ready"), sem("wqs_ready")
        fills_ready = sem("fills_ready")
        mv_ready = [sem(f"mv_ready{i}") for i in range(3)]
        vareps_ready = [sem(f"vareps_ready{i}") for i in range(3)]
        rstd_ready = [sem(f"rstd_ready{i}") for i in range(3)]
        stats_ready = [sem(f"stats_ready{i}") for i in range(3)]
        power_ready, warm_ready, hs_ready, hb_ready = (sem(n) for n in (
            "power_ready", "warm_ready", "hs_ready", "hb_ready"))
        erec_ready, og_ready, h1_ready = sem("erec_ready"), sem("og_ready"), sem("h1_ready")
        xc_ready, cmax_ready = sem("xc_ready"), sem("cmax_ready")
        ex_sb_act, y_sb_act = sem("ex_sb_act"), sem("y_sb_act")
        h_mm, hn_ready = sem("h_mm"), sem("hn_ready")
        hnT_mm, hnT_sb, qkv_mm, qk_sb, v_sb, vo_mm, vo_sb = (sem(n) for n in (
            "hnT_mm", "hnT_sb", "qkv_mm", "qk_sb", "v_sb", "vo_mm", "vo_sb"))
        s_mm, nmax_ready, prob_ready = (sem(n) for n in ("s_mm", "nmax_ready", "prob_ready"))
        probT_mm, probT_sb = sem("probT_mm"), sem("probT_sb")
        o_mm, o_sb, xn_ready, xcT_mm, xcT_sb = (sem(n) for n in ("o_mm", "o_sb", "xn_ready", "xcT_mm", "xcT_sb"))
        lg_mm, gnmax_ready, gexp_ready = sem("lg_mm"), sem("gnmax_ready"), sem("gexp_ready")
        G_ready, GT_mm, slotT_ready, slot_mm, pick_ready = (sem(n) for n in (
            "G_ready", "GT_mm", "slotT_ready", "slot_mm", "pick_ready"))
        Gimg_ready, identb_ready = sem("Gimg_ready"), sem("identb_ready")
        xhi_ready, xleft_ready, xmid_ready, xlo_ready = (sem(n) for n in (
            "xhi_ready", "xleft_ready", "xmid_ready", "xlo_ready"))
        wpick_ready, ex_mm, ex_sb = sem("wpick_ready"), sem("ex_mm"), sem("ex_sb")
        hid_mm, hid_sb, y_mm, yT_sb = sem("hid_mm"), sem("hid_sb"), sem("y_mm"), sem("yT_sb")
        yt_mm, y_sb, put_mm, put_sb = sem("yt_mm"), sem("y_sb"), sem("put_mm"), sem("put_sb")
        res_mm, res_ready = sem("res_mm"), sem("res_ready")

        ident = cf[:, C_ID:C_ID + 128]

        def sel(item, n):
            return ch[:, H_SEL + item:H_SEL + item + 1].broadcast_to([BR, n])

        FULL = sum(n == TILE_B for n in NB)
        PICKS = [(0, 3), (3, FULL - 3)] + [(t, 1) for t in range(FULL, TILES)]
        FIRST_PICKED = [t for t, _ in PICKS]
        GROUPS = [(0, FULL - 1, P), (FULL - 1, 1, P)] + [(t, 1, NT[t]) for t in range(FULL, TILES)]
        SPANS = [(0, FULL, SL)] + [(t, 1, NB[t] * TOPK) for t in range(FULL, TILES)]

        EARLY = FULL - 1
        EX_TILES = BANK // (EH * SL)
        EX_REST = [(t, 1, NB[t] * TOPK) for t in range(EX_TILES, TILES)]

        def slot_cols(buf, t, k, w):
            return buf[0:NT[t], t * E * SL:t * E * SL + k * E * w].rearrange("p (r w) -> p r w", w=w)

        def by_tile(buf, t, k, w):
            return buf[:, t * E * SL:t * E * SL + k * E * w].rearrange("p (t e w) -> p t e w", t=k, e=E)

        def half_cols(t, h, w):
            return slice(t * E * SL + h * EH * w, t * E * SL + (h + 1) * EH * w)

        FILL_BANK = 0
        TOP_BANK, EX_BANK, HID_BANK, Y_BANK = 4, ((1, 2), (3, 7)), (4, 5, 6, 0, 1, 2), (3, 7, 4)
        PUT_BANK, YT_BANK, RES_BANK = (5, 6, 0), (1, 2, 5, 6, 0, 3), (7, 4, 1, 2, 5, 6)

        def ex_copy(copy, h, part):
            for t, k, w in ((0, EX_TILES, SL),) if part == 0 else EX_REST:
                c0 = (t - part * EX_TILES) * EH * SL
                last = copy(exT[:, EH * h:EH * (h + 1), t * SL:t * SL + k * w].rearrange("p e (t w) -> p t e w", t=k),
                            bank[EX_BANK[h][part]][:, c0:c0 + k * EH * w].rearrange("p (t e w) -> p t e w", t=k, e=EH))
            return last

        def add_b2(j):
            e0, k = PER_BANK * j, min(PER_BANK, E - PER_BANK * j)
            src = bank[Y_BANK[j]][:, 0:k * NS].rearrange("p (e n) -> p e n", e=k)
            b2 = xb[:, X_B2 + e0:X_B2 + e0 + k].unsqueeze(2)
            for t, m, w in SPANS:
                last = nc.vector.tensor_tensor(by_tile(yT, t, m, w)[:, :, e0:e0 + k, :].rearrange("p t e w -> p e t w"),
                                               src[:, :, t * SL:t * SL + m * w].rearrange("p e (t w) -> p e t w", t=m),
                                               b2.unsqueeze(3).broadcast_to([128, k, m, w]), ALU.add)
            return last

        def y_copy(copy, t):
            w = EH * NB[t] * TOPK
            return copy(y[0:w, 2 * t:2 * t + 2, :].rearrange("p b d -> p (b d)"), bank[YT_BANK[t]][0:w, 0:2 * D])

        block = ctx.enter_context(nc.Block())

        @block.sync
        def _(sp):
            half = KCH // 2
            for i in range(2):
                w_cols = slice(i * half * D, (i + 1) * half * D)
                x_cols = slice(i * half * NT[0], (i + 1) * half * NT[0])
                sp.dma_start(wt[:, w_cols], w_tok[:, w_cols]).then_inc(in_wt[i], 16)
                sp.dma_start(xp[0][:, x_cols], patches[:, x_cols]).then_inc(in_x0[i], 16)
            sp.dma_start(chf[:, :], const_h).then_inc(in_ch, 16)
            for t in range(1, TILES):
                at_col = KCH * sum(NT[:t])
                sp.dma_start(xp[t][:, :], patches[:, at_col:at_col + KCH * NT[t]]).then_inc(in_x[t], 16)
                if t == 1:
                    sp.dma_start(cf[:, :], const_f).then_inc(in_cf, 16)
                    sp.dma_start(wqkvo[:, :], w_qkvo).then_inc(in_qkvo, 16)
                    sp.dma_start(xb[:, :], feature_biases).then_inc(in_xb, 16)
                if t == 2:
                    sp.dma_start(gam[:, :], gamma.partition_broadcast(P)).then_inc(in_gb, 16)
                    sp.dma_start(bet[:, :], beta.partition_broadcast(P)).then_inc(in_gb, 16)
                    sp.dma_start(wg[:, :], w_gate).then_inc(in_wg, 16)
            sp.dma_start(w1s[:, :, :], w1).then_inc(in_w1, 16)
            sp.dma_start(w2s[:, :, :, :], w2).then_inc(in_w2, 16)
            t = 0
            while t < TILES:
                k = 2 if t + 2 < FULL else 1
                row = sum(NT[:t])
                sp.wait_ge(res_ready, t + k)
                if k == 2:
                    sp.dma_start(out[row:row + 2 * P, :].rearrange("(t p) d -> p t d", t=2),
                                 res[:, t:t + 2, :]).then_inc(out_done, 16)
                else:
                    sp.dma_start(out[row:row + NT[t], :], res[0:NT[t], t, :]).then_inc(out_done, 16)
                t += k
            sp.wait_ge(out_done, 16 * (TILES - FULL // 2))

        @block.gpsimd
        def _(pool):
            pool.dma_start(braw[:, :], bias_rows).then_inc(in_bias, 16)
            nc.gpsimd.memset(power[:, :], -0.5).then_inc(power_ready, 1)
            nc.gpsimd.memset(ninth[:, :], -1.0).then_inc(fills_ready, 1)
            nc.gpsimd.memset(Gimg[:, :], 0.0).then_inc(fills_ready, 1)
            pool.wait_ge(power_ready, 1)

            def add_eps(t, which, eps):
                pool.wait_ge(mv_ready[which], t + 1)
                nc.gpsimd.tensor_scalar(vareps[0:NT[t], t, which:which + 1], mv[0:NT[t], t, which, 1:2],
                                        eps, None, ALU.add).then_inc(vareps_ready[which], 1)

            def inv_sqrt(t, which):
                pool.wait_ge(vareps_ready[which], t + 1)
                nc.gpsimd.tensor_tensor(rstd[0:NT[t], t, which:which + 1], vareps[0:NT[t], t, which:which + 1],
                                        power[0:NT[t], :], ALU.pow).then_inc(rstd_ready[which], 1)

            def add_eps_pre(t):
                add_eps(t, 0, EPS_PRE)

            def inv_sqrt_pre(t):
                inv_sqrt(t, 0)

            def add_eps_attn(t):
                add_eps(t, 1, EPS_ATTN)

            def inv_sqrt_attn(t):
                inv_sqrt(t, 1)

            def add_eps_ffn(t):
                add_eps(t, 2, EPS_PRE)

            def inv_sqrt_ffn(t):
                inv_sqrt(t, 2)

            def residual_beta(t):
                pool.wait_ge(hs_ready, t + 1)
                if t == 0:
                    pool.wait_ge(in_gb, 32)
                nc.gpsimd.tensor_tensor(hb[0:NT[t], t, :], hs[0:NT[t], t, :], bet[0:NT[t], :],
                                        ALU.add).then_inc(hb_ready, 1)

            def rest_of_high(g):
                t, k, n = GROUPS[g]
                pool.wait_ge(xhi_ready, g + 1)
                nc.gpsimd.tensor_tensor(xleft[0:n, t:t + k, :], xn[0:n, t:t + k, :], xpart[0:n, 0, t:t + k, :],
                                        ALU.subtract).then_inc(xleft_ready, 1)

            def low_part(g):
                t, k, n = GROUPS[g]
                pool.wait_ge(xmid_ready, g + 1)
                nc.gpsimd.tensor_tensor(xpart[0:n, 2, t:t + k, :], xleft[0:n, t:t + k, :], xpart[0:n, 1, t:t + k, :],
                                        ALU.subtract).then_inc(xlo_ready, 1)

            add_eps_pre(0); inv_sqrt_pre(0); add_eps_pre(1); inv_sqrt_pre(1); add_eps_pre(2); inv_sqrt_pre(2)
            residual_beta(0); add_eps_pre(3); inv_sqrt_pre(3); residual_beta(1); add_eps_attn(0)
            inv_sqrt_attn(0); residual_beta(2); add_eps_pre(4); inv_sqrt_pre(4); add_eps_ffn(0); add_eps_attn(1)
            inv_sqrt_attn(1); inv_sqrt_ffn(0); add_eps_pre(5); inv_sqrt_pre(5); residual_beta(3); add_eps_ffn(1)
            add_eps_attn(2); inv_sqrt_attn(2); residual_beta(4); inv_sqrt_ffn(1); residual_beta(5)
            add_eps_attn(3); inv_sqrt_attn(3); add_eps_ffn(2); inv_sqrt_ffn(2); add_eps_attn(4)
            inv_sqrt_attn(4); add_eps_ffn(3); inv_sqrt_ffn(3); add_eps_attn(5); inv_sqrt_attn(5); add_eps_ffn(4)
            inv_sqrt_ffn(4); add_eps_ffn(5); inv_sqrt_ffn(5)

            rest_of_high(0)
            rest_of_high(1)
            low_part(0)
            rest_of_high(2)
            low_part(1)
            low_part(2)

            pool.wait_ge(G_ready, TILES - EARLY)
            pool.wait_ge(pick_ready, 2 * len(PICKS))
            for t, k, w in SPANS:
                last = nc.gpsimd.tensor_tensor(
                    slot_cols(wpick, t, k, w), slot_cols(pick, t, k, w),
                    G[0:NT[t], t:t + k, :].rearrange("p t e -> p (t e)").unsqueeze(2).broadcast_to([NT[t], k * E, w]),
                    ALU.mult)
            last.then_inc(wpick_ready, 1)

        @block.scalar
        def _(act):
            def hnT_copy(t):
                act.wait_ge(hnT_mm, t + 1)
                nc.scalar.activation(hnT[:, t, 0:NT[t]], bank[2][:, 0:NT[t]], ACT.Copy).then_inc(hnT_sb, 1)

            def bias_relu(t, i, bias):
                return nc.scalar.activation(qkv[:, t, i * NT[t]:(i + 1) * NT[t]], bank[3][:, i * NT[t]:(i + 1) * NT[t]],
                                            ACT.Relu, bias=bias)

            def q_relu(t):
                act.wait_ge(qkv_mm, t + 1)
                if t == 0:
                    act.wait_ge(in_xb, 16)
                    act.wait_ge(wqs_ready, 2)
                bias_relu(t, 0, bqs[:, :]).then_inc(qk_sb, 1)

            def k_relu(t):
                act.wait_ge(qkv_mm, t + 1)
                bias_relu(t, 1, xb[:, X_K:X_K + 1]).then_inc(qk_sb, 1)

            def v_relu(t):
                act.wait_ge(qkv_mm, t + 1)
                bias_relu(t, 2, xb[:, X_V:X_V + 1]).then_inc(v_sb, 1)

            def vo_copy(t):
                act.wait_ge(vo_mm, t + 1)
                nc.scalar.activation(vo[0:NT[t], t, :], bank[5][0:NT[t], 128:256], ACT.Copy).then_inc(vo_sb, 1)

            def h_copy(t):
                act.wait_ge(hn_ready, t + 1)
                nc.scalar.activation(hs[0:NT[t], t, :], bank[t % 2][0:NT[t], 0:D], ACT.Copy).then_inc(hs_ready, 1)

            def softmax_exp(t):
                act.wait_ge(nmax_ready, t + 1)
                nc.scalar.activation(prob[0:NT[t], t, 0:NT[t]], bank[4][0:NT[t], 0:NT[t]], ACT.Exp,
                                     bias=nmax[0:NT[t], t:t + 1],
                                     accum_out=esum[0:NT[t], t:t + 1]).then_inc(prob_ready, 1)

            def probT_copy(t):
                act.wait_ge(probT_mm, t + 1)
                nc.scalar.activation(probT[0:NT[t], t, 0:NT[t]], bank[5][0:NT[t], 0:NT[t]],
                                     ACT.Copy).then_inc(probT_sb, 1)

            def o_relu(t):
                act.wait_ge(o_mm, t + 1)
                act.wait_ge(erec_ready, t + 1)
                nc.scalar.activation(o[0:NT[t], t, :], bank[6][0:NT[t], 0:D], ACT.Relu,
                                     scale=erec[0:NT[t], t:t + 1]).then_inc(o_sb, 1)

            def xcT_copy(t):
                act.wait_ge(xcT_mm, t + 1)
                nc.scalar.activation(xcT[:, t, 0:NT[t]], bank[2][:, 128:128 + NT[t]], ACT.Copy).then_inc(xcT_sb, 1)

            def gate_exp(t):
                act.wait_ge(gnmax_ready, t + 1)
                act.wait_ge(rstd_ready[2], t + 1)
                nc.scalar.activation(gexp[0:NT[t], t, :], bank[7][0:NT[t], E * t:E * t + E], ACT.Exp,
                                     bias=gnmax[0:NT[t], t:t + 1], scale=rstd[0:NT[t], t, 2:3],
                                     accum_out=gsum[0:NT[t], t:t + 1]).then_inc(gexp_ready, 1)

            def ffn_norm(t):
                act.wait_ge(xc_ready, t + 1)
                act.wait_ge(rstd_ready[2], t + 1)
                nc.scalar.activation(xn[0:NT[t], t, :], xc[0:NT[t], t, :], ACT.Copy,
                                     scale=rstd[0:NT[t], t, 2:3]).then_inc(xn_ready, 1)

            def high_part(g):
                t, k, n = GROUPS[g]
                act.wait_ge(xn_ready, t + k)
                nc.scalar.activation(xpart[0:n, 0, t:t + k, :], xn[0:n, t:t + k, :], ACT.Copy).then_inc(xhi_ready, 1)

            def mid_part(g):
                t, k, n = GROUPS[g]
                act.wait_ge(xleft_ready, g + 1)
                nc.scalar.activation(xpart[0:n, 1, t:t + k, :], xleft[0:n, t:t + k, :],
                                     ACT.Copy).then_inc(xmid_ready, 1)

            h_copy(0); hnT_copy(0); h_copy(1); q_relu(0); hnT_copy(1); k_relu(0); v_relu(0); softmax_exp(0)
            q_relu(1); vo_copy(0); h_copy(2); v_relu(1); k_relu(1); hnT_copy(2); probT_copy(0); softmax_exp(1)
            vo_copy(1); o_relu(0); k_relu(2); q_relu(2); probT_copy(1); h_copy(3); hnT_copy(3); v_relu(2)
            softmax_exp(2); o_relu(1); vo_copy(2); v_relu(3); k_relu(3); probT_copy(2); h_copy(4); q_relu(3)
            hnT_copy(4); vo_copy(3); o_relu(2); xcT_copy(0); softmax_exp(3); k_relu(4); q_relu(4); probT_copy(3)
            v_relu(4); h_copy(5); hnT_copy(5); gate_exp(0); o_relu(3); vo_copy(4); xcT_copy(1); softmax_exp(4)
            k_relu(5); q_relu(5); v_relu(5); probT_copy(4); gate_exp(1); ffn_norm(0); o_relu(4); xcT_copy(2)
            softmax_exp(5); vo_copy(5); probT_copy(5); gate_exp(2); xcT_copy(3); o_relu(5); ffn_norm(1)
            ffn_norm(2); gate_exp(3); xcT_copy(4); ffn_norm(3); high_part(0); ffn_norm(4); gate_exp(4)
            xcT_copy(5); high_part(1); gate_exp(5); mid_part(0); ffn_norm(5)
            mid_part(1)
            high_part(2)
            mid_part(2)
            nc.scalar.preload_act_table(ACT.Gelu)

            act.wait_ge(ex_mm, 1)
            ex_copy(nc.scalar.copy, 0, 0).then_inc(ex_sb_act, 1)
            act.wait_ge(ex_mm, 4)
            ex_copy(nc.scalar.copy, 1, 1).then_inc(ex_sb_act, 1)
            for k in range(HID_BANKS):
                act.wait_ge(hid_mm, k + 1)
                for ec in range(PER_BANK * k, min(PER_BANK * (k + 1), EC)):
                    c0 = (ec - PER_BANK * k) * NS
                    nc.scalar.activation(hid[:, ec * NS:(ec + 1) * NS], bank[HID_BANK[k]][:, c0:c0 + NS], ACT.Gelu,
                                         bias=xb[:, X_B1 + ec:X_B1 + ec + 1]).then_inc(hid_sb, 1)
            for t in range(1, TILES, 2):
                act.wait_ge(yt_mm, t + 1)
                y_copy(nc.scalar.copy, t).then_inc(y_sb_act, 1)

        @block.vector
        def _(dve):
            done = [0]

            def chain(ins):
                done[0] += 1
                ins.then_inc(dve_done, 1)
                dve.wait_ge(dve_done, done[0])

            def stats_of(src, t, which):
                nc.vector.bn_stats(stats[0:NT[t], t, which, :], src).then_inc(stats_ready[which], 1)

            def mean_var(t, which):
                dve.wait_ge(stats_ready[which], t + 1)
                nc.vector.bn_aggr(mv[0:NT[t], t, which, :], stats[0:NT[t], t, which, :]).then_inc(mv_ready[which], 1)

            def normalise(dst, src, t, which):
                dve.wait_ge(mv_ready[which], t + 1)
                dve.wait_ge(rstd_ready[which], t + 1)
                return nc.vector.tensor_scalar(dst, src, mv[0:NT[t], t, which, 0:1],
                                               rstd[0:NT[t], t, which:which + 1], ALU.subtract, ALU.mult)

            nc.vector.memset(warm[:, :], 0.0).then_inc(warm_ready, 1)
            dve.wait_ge(in_bias, 16)
            chain(nc.vector.tensor_copy(bhi[:, :], braw[:, 0:D]))
            chain(nc.vector.tensor_tensor(bres1[:, :], braw[:, 0:D], bhi[:, :], ALU.subtract))
            chain(nc.vector.tensor_copy(bmid[:, :], bres1[:, :]))
            chain(nc.vector.tensor_tensor(bres2[:, :], bres1[:, :], bmid[:, :], ALU.subtract))
            chain(nc.vector.tensor_scalar(bsum1[:, :], bhi[:, :], braw[:, D:D + 1], None, ALU.mult))
            chain(nc.vector.scalar_tensor_tensor(bsum2[:, :], bmid[:, :], braw[:, D + 1:D + 2], bsum1[:, :],
                                                 ALU.mult, ALU.add))
            nc.vector.scalar_tensor_tensor(biases[:, :], bres2[:, :], braw[:, D + 2:D + 3], bsum2[:, :],
                                           ALU.mult, ALU.add).then_inc(biases_ready, 1)
            dve.wait_ge(in_ch, 16)
            nc.vector.tensor_copy(ch[:, :], chf[:, :]).then_inc(ch_ready, 1)
            def projection_constants():
                dve.wait_ge(in_cf, 16)
                nc.vector.tensor_copy(identb[:, :], ident).then_inc(identb_ready, 1)
                nc.vector.tensor_copy(slotb[:, :], cf[0:P, C_SLOT:C_SLOT + EH * SL]).then_inc(dve_done, 1)
                done[0] += 1
                dve.wait_ge(in_qkvo, 16)
                nc.vector.tensor_scalar(wqs[:, :], wqkvo[:, 0:D], SCALE, None, ALU.mult).then_inc(wqs_ready, 1)
                dve.wait_ge(in_xb, 16)
                nc.vector.tensor_scalar(bqs[:, :], xb[:, X_Q:X_Q + 1], SCALE, None, ALU.mult).then_inc(wqs_ready, 1)

            def h_stats(t):
                dve.wait_ge(h_mm, t + 1)
                stats_of(bank[t % 2][0:NT[t], 0:D], t, 0)

            def h_mean_var(t):
                mean_var(t, 0)

            def pre_norm(t):
                normalise(hn[0:NT[t], t, :], bank[t % 2][0:NT[t], 0:D], t, 0).then_inc(hn_ready, 1)

            def row_max(t):
                dve.wait_ge(s_mm, t + 1)
                nc.vector.tensor_reduce(nmax[0:NT[t], t:t + 1], bank[4][0:NT[t], 0:NT[t]], AX.X, ALU.max,
                                        negate=True).then_inc(nmax_ready, 1)

            def row_recip(t):
                dve.wait_ge(prob_ready, t + 1)
                nc.vector.reciprocal(erec[0:NT[t], t:t + 1], esum[0:NT[t], t:t + 1]).then_inc(erec_ready, 1)

            def o_stats(t):
                dve.wait_ge(o_sb, t + 1)
                stats_of(o[0:NT[t], t, :], t, 1)

            def o_mean_var(t):
                mean_var(t, 1)

            def o_gamma(t):
                dve.wait_ge(mv_ready[1], t + 1)
                if t == 0:
                    dve.wait_ge(in_gb, 32)
                nc.vector.scalar_tensor_tensor(og[0:NT[t], t, :], o[0:NT[t], t, :], mv[0:NT[t], t, 1, 0:1],
                                               gam[0:NT[t], :], ALU.subtract, ALU.mult).then_inc(og_ready, 1)

            def o_residual(t):
                dve.wait_ge(og_ready, t + 1)
                dve.wait_ge(rstd_ready[1], t + 1)
                dve.wait_ge(hb_ready, t + 1)
                nc.vector.scalar_tensor_tensor(h1[0:NT[t], t, :], og[0:NT[t], t, :], rstd[0:NT[t], t, 1:2],
                                               hb[0:NT[t], t, :], ALU.mult, ALU.add).then_inc(h1_ready, 1)

            def h1_stats(t):
                dve.wait_ge(h1_ready, t + 1)
                stats_of(h1[0:NT[t], t, :], t, 2)

            def h1_mean_var(t):
                mean_var(t, 2)

            def centre(t):
                dve.wait_ge(mv_ready[2], t + 1)
                nc.vector.tensor_scalar(xc[0:NT[t], t, :], h1[0:NT[t], t, :], mv[0:NT[t], t, 2, 0:1], None,
                                        ALU.subtract).then_inc(xc_ready, 1)

            def gate_max(t):
                dve.wait_ge(lg_mm, t + 1)
                nc.vector.tensor_reduce(cmax[0:NT[t], t:t + 1], bank[7][0:NT[t], E * t:E * t + E], AX.X, ALU.max,
                                        negate=True).then_inc(cmax_ready, 1)

            def gate_max_scale(t):
                dve.wait_ge(cmax_ready, t + 1)
                dve.wait_ge(rstd_ready[2], t + 1)
                nc.vector.tensor_scalar(gnmax[0:NT[t], t:t + 1], cmax[0:NT[t], t:t + 1], rstd[0:NT[t], t, 2:3], None,
                                        ALU.mult).then_inc(gnmax_ready, 1)

            def first_gates():
                n = EARLY
                dve.wait_ge(gexp_ready, n)
                chain(nc.vector.reciprocal(grec[:, 0:n], gsum[:, 0:n]))
                chain(nc.vector.tensor_tensor(G[:, 0:n, :], gexp[:, 0:n, :],
                                              grec[:, 0:n].unsqueeze(2).broadcast_to([P, n, E]), ALU.mult))
                dve.wait_ge(fills_ready, 2)
                step_cols = RT + TILE_B * E
                dst = Gimg[:, 0:n * step_cols].rearrange("p (t c) -> p t c", c=step_cols)[:, :, 0:TILE_B * E]
                nc.vector.tensor_tensor(dst.rearrange("p t (e b) -> p t e b", b=TILE_B),
                                        G[:, 0:n, :].unsqueeze(3).broadcast_to([P, n, E, TILE_B]),
                                        cf[0:P, C_IMG:C_IMG + TILE_B].unsqueeze(1).unsqueeze(1)
                                        .broadcast_to([P, n, E, TILE_B]), ALU.mult).then_inc(Gimg_ready, 1)

            def late_gates(t):
                n, nb = NT[t], NB[t]
                c0 = t * RT + t * TILE_B * E
                dve.wait_ge(gexp_ready, t + 1)
                chain(nc.vector.reciprocal(grec[0:n, t:t + 1], gsum[0:n, t:t + 1]))
                nc.vector.scalar_tensor_tensor(
                    Gimg[0:n, c0:c0 + E * nb].rearrange("p (e b) -> p e b", b=nb),
                    gexp[0:n, t, :].unsqueeze(2).broadcast_to([n, E, nb]), grec[0:n, t:t + 1],
                    cf[0:n, C_IMG:C_IMG + nb].unsqueeze(1).broadcast_to([n, E, nb]),
                    ALU.mult, ALU.mult).then_inc(Gimg_ready, 1)

            h_stats(0); h_mean_var(0)
            projection_constants()
            pre_norm(0); h_stats(1); h_mean_var(1); pre_norm(1); h_stats(2)
            h_mean_var(2); row_max(0); pre_norm(2); row_recip(0); h_stats(3); h_mean_var(3); row_max(1)
            pre_norm(3); row_recip(1); o_stats(0); o_mean_var(0); h_stats(4); row_max(2); o_gamma(0)
            h_mean_var(4); o_residual(0); o_stats(1); h1_stats(0); o_mean_var(1); h1_mean_var(0); centre(0)
            pre_norm(4); row_recip(2); o_gamma(1); h_stats(5); o_residual(1); h_mean_var(5); h1_stats(1)
            row_max(3); o_stats(2); o_mean_var(2); h1_mean_var(1); row_recip(3); pre_norm(5); o_gamma(2)
            gate_max(0); gate_max_scale(0); centre(1); row_max(4); o_residual(2); h1_stats(2); o_stats(3)
            h1_mean_var(2); o_mean_var(3); centre(2); row_recip(4); gate_max(1); gate_max_scale(1); o_gamma(3)
            o_residual(3); h1_stats(3); row_max(5); h1_mean_var(3); o_stats(4); o_mean_var(4); centre(3)
            gate_max(2); gate_max_scale(2); o_gamma(4); row_recip(5); o_residual(4); h1_stats(4); o_stats(5)
            h1_mean_var(4); o_mean_var(5); gate_max(3); centre(4); gate_max_scale(3); o_gamma(5); o_residual(5)
            h1_stats(5); gate_max(4); h1_mean_var(5); gate_max_scale(4); centre(5)
            first_gates(); late_gates(4); gate_max(5)
            gate_max_scale(5)

            late_gates(TILES - 1)
            for t in range(EARLY, TILES):
                n = NT[t]
                nc.vector.tensor_scalar(G[0:n, t, :], gexp[0:n, t, :], grec[0:n, t:t + 1], None,
                                        ALU.mult).then_inc(G_ready, 1)

            dve.wait_ge(GT_mm, 1)
            GT = bank[TOP_BANK][0:RT, 0:S]
            chain(nc.vector.max(top8[:, :], GT))
            chain(nc.vector.match_replace(left8[:, :], top8[:, :], GT, -1.0))
            chain(nc.vector.tensor_reduce(ninth[:, 0:1], left8[:, :], AX.X, ALU.max))
            chain(nc.vector.match_replace(left9[:, :], ninth[:, :], left8[:, :], -1.0))
            chain(nc.vector.tensor_scalar(chosen[:, :], left9[:, :], 0.0, None, ALU.is_lt))
            chain(nc.vector.tensor_tensor_scan(count[:, :], chosen[:, :], chosen[:, :], 0.0, ALU.add, ALU.max))
            nc.vector.tensor_tensor(slotT[:, :, :], count[:, :].unsqueeze(1).broadcast_to([RT, TILE_B, S]),
                                    chosen[:, :].unsqueeze(1).broadcast_to([RT, TILE_B, S]),
                                    ALU.mult).then_inc(slotT_ready, 1)

            dve.wait_ge(slot_mm, 1)
            slot = bank[TOP_BANK][0:P, 128:128 + RT]
            for h in range(2):
                for t, k in PICKS:
                    n, nb, w = NT[t], NB[t], NB[t] * TOPK
                    rows = slice(t * E * TILE_B, t * E * TILE_B + k * E * nb)
                    if nb == TILE_B:
                        mine, numbers = EH * TILE_B, slotb[0:n, :].rearrange("p (r w) -> p r w", w=TOPK)
                    else:
                        mine, numbers = EH, slotb[0:n, :].rearrange("p (e w) -> p e w", w=SL)[:, :, 0:TOPK]
                    nc.vector.tensor_tensor(
                        pick[0:n, t * E * SL:t * E * SL + k * E * w].rearrange(
                            "p (t r w) -> p t r w", t=k, w=TOPK)[:, :, h * mine:(h + 1) * mine, :],
                        slot[0:n, rows].rearrange("p (t r) -> p t r", t=k)[:, :, h * mine:(h + 1) * mine].unsqueeze(3)
                        .broadcast_to([n, k, mine, TOPK]),
                        numbers.unsqueeze(1).broadcast_to([n, k, mine, TOPK]), ALU.is_equal).then_inc(pick_ready, 1)

            dve.wait_ge(ex_mm, 2)
            ex_copy(nc.vector.tensor_copy, 0, 1).then_inc(ex_sb, 1)
            dve.wait_ge(ex_mm, 3)
            ex_copy(nc.vector.tensor_copy, 1, 0).then_inc(ex_sb, 1)

            for p in range(PAIRS):
                dve.wait_ge(put_mm, p + 1)
                for t in (2 * p, 2 * p + 1):
                    w, n = EH * NB[t] * TOPK, NT[t]
                    src = bank[PUT_BANK[p]][0:w, (t % 2) * 2 * P:(t % 2) * 2 * P + 2 * P]
                    last = nc.vector.tensor_copy(put[0:w, 2 * t:2 * t + 2, 0:n],
                                                 src.rearrange("w (h n) -> w h n", h=2)[:, :, 0:n])
                last.then_inc(put_sb, 1)

            dve.wait_ge(in_xb, 16)
            for j in range(Y_BANKS):
                dve.wait_ge(y_mm, j + 1)
                add_b2(j).then_inc(yT_sb, 1)

            for t in range(0, TILES, 2):
                dve.wait_ge(yt_mm, t + 1)
                y_copy(nc.vector.tensor_copy, t).then_inc(y_sb, 1)

            for t in range(TILES):
                dve.wait_ge(res_mm, t + 1)
                nc.vector.tensor_tensor(res[0:NT[t], t, :], bank[RES_BANK[t]][0:NT[t], 0:D],
                                        h1[0:NT[t], t, :], ALU.add).then_inc(res_ready, 1)

        @block.tensor
        def _(pe):
            def embed(t, part):
                h = bank[t % 2][0:NT[t], 0:D]
                n = NT[t]
                if t == 0 and part < 2:
                    pe.wait_ge(in_wt[part], 16)
                    pe.wait_ge(in_x0[part], 16)
                if t >= 1 and part == 0:
                    pe.wait_ge(in_x[t], 16)
                if t >= 2 and part == 0:
                    pe.wait_ge(hs_ready, t - 1)
                for c in range(2 * part, 2 * part + 2):
                    nc.tensor.matmul(h, xp[t][:, c * n:(c + 1) * n], wt[:, c * D:(c + 1) * D],
                                     start=(c == 0), stop=False)
                if part == 2:
                    if t == 0:
                        pe.wait_ge(ch_ready, 1)
                        pe.wait_ge(biases_ready, 1)
                    nc.tensor.matmul(h, ch[:, H_TOK:H_TOK + n], biases[:, :], start=False,
                                     stop=True).then_inc(h_mm, 1)

            def hn_transpose(t, xc_before):
                pe.wait_ge(hn_ready, t + 1)
                if t == 0:
                    pe.wait_ge(in_cf, 16)
                if t >= 1:
                    pe.wait_ge(hnT_sb, t)
                if xc_before >= 1:
                    pe.wait_ge(xcT_sb, xc_before)
                nc.tensor.transpose(bank[2][:, 0:NT[t]], hn[0:NT[t], t, :], ident[0:NT[t], 0:NT[t]]).then_inc(hnT_mm, 1)

            def queries_keys_values(t):
                n = NT[t]
                pe.wait_ge(hnT_sb, t + 1)
                if t == 0:
                    pe.wait_ge(in_qkvo, 16)
                    pe.wait_ge(wqs_ready, 1)
                if t >= 1:
                    pe.wait_ge(qk_sb, 2 * t)
                    pe.wait_ge(v_sb, t)
                for i, w in enumerate((wqs[:, :], wqkvo[:, D:2 * D], wqkvo[:, 2 * D:3 * D])):
                    last = nc.tensor.matmul(bank[3][:, i * n:(i + 1) * n], w, hnT[:, t, 0:n], start=True, stop=True)
                last.then_inc(qkv_mm, 1)

            def values_out(t):
                n = NT[t]
                pe.wait_ge(v_sb, t + 1)
                if t >= 1:
                    pe.wait_ge(probT_sb, t)
                nc.tensor.matmul(bank[5][0:n, 128:256], qkv[:, t, 2 * n:3 * n], wqkvo[:, 3 * D:4 * D],
                                 start=True, stop=False)
                nc.tensor.matmul(bank[5][0:n, 128:256], sel(I_O, n), biases[:, :], start=False,
                                 stop=True).then_inc(vo_mm, 1)

            def scores(t):
                n = NT[t]
                pe.wait_ge(qk_sb, 2 * (t + 1))
                if t >= 1:
                    pe.wait_ge(prob_ready, t)
                s = bank[4][0:n, 0:n]
                nc.tensor.matmul(s, ch[:, H_ML:H_ML + n], ch[:, H_MR:H_MR + n], start=True, stop=False)
                nc.tensor.matmul(s, qkv[:, t, 0:n], qkv[:, t, n:2 * n], start=False, stop=True).then_inc(s_mm, 1)

            def prob_transpose(t):
                n = NT[t]
                pe.wait_ge(prob_ready, t + 1)
                pe.wait_ge(vo_sb, t + 1)
                nc.tensor.transpose(bank[5][0:n, 0:n], prob[0:n, t, 0:n], ident[0:n, 0:n]).then_inc(probT_mm, 1)

            def attend(t):
                n = NT[t]
                pe.wait_ge(probT_sb, t + 1)
                if t >= 1:
                    pe.wait_ge(o_sb, t)
                nc.tensor.matmul(bank[6][0:n, 0:D], probT[0:n, t, 0:n], vo[0:n, t, :], start=True,
                                 stop=True).then_inc(o_mm, 1)

            def xc_transpose(t, hn_before):
                pe.wait_ge(xc_ready, t + 1)
                pe.wait_ge(hnT_sb, hn_before)
                if t >= 1:
                    pe.wait_ge(xcT_sb, t)
                nc.tensor.transpose(bank[2][:, 128:128 + NT[t]], xc[0:NT[t], t, :],
                                    ident[0:NT[t], 0:NT[t]]).then_inc(xcT_mm, 1)

            def gate(t):
                pe.wait_ge(xcT_sb, t + 1)
                if t == 0:
                    pe.wait_ge(in_wg, 16)
                else:
                    pe.wait_ge(gexp_ready, t)
                nc.tensor.matmul(bank[7][0:NT[t], E * t:E * t + E], xcT[:, t, 0:NT[t]], wg[:, :], start=True,
                                 stop=True).then_inc(lg_mm, 1)

            def fill(count):
                for _ in range(count):
                    nc.tensor.matmul(bank[FILL_BANK][:, :], warm[:, 0:128], warm[:, :], start=True, stop=True)

            def image_gates(t):
                ins = nc.tensor.matmul(bank[TOP_BANK][0:RT, 0:S], Gimg[0:NT[t], t * RT:(t + 1) * RT],
                                       cf[0:NT[t], C_POS:C_POS + S], start=t == 0, stop=t == TILES - 1)
                if t == TILES - 1:
                    ins.then_inc(GT_mm, 1)

            pe.wait_ge(warm_ready, 1)
            fill(WARM_START)
            embed(0, 0); embed(0, 1); embed(0, 2); embed(1, 0); embed(1, 1); embed(1, 2); hn_transpose(0, 0)
            embed(2, 0); queries_keys_values(0); embed(2, 1); hn_transpose(1, 0); embed(2, 2); embed(3, 0)
            scores(0); queries_keys_values(1); values_out(0); embed(3, 1); embed(3, 2); hn_transpose(2, 0)
            prob_transpose(0); embed(4, 0); scores(1); attend(0); values_out(1); queries_keys_values(2)
            embed(4, 1); prob_transpose(1); embed(4, 2); hn_transpose(3, 0); scores(2); attend(1); embed(5, 0)
            values_out(2); queries_keys_values(3); prob_transpose(2); embed(5, 1); embed(5, 2)
            hn_transpose(4, 0); values_out(3); attend(2); scores(3); xc_transpose(0, 5); queries_keys_values(4)
            gate(0); prob_transpose(3)
            pe.wait_ge(hs_ready, TILES - 1)
            fill(1); hn_transpose(5, 1); scores(4); attend(3); values_out(4)
            xc_transpose(1, 6); queries_keys_values(5); gate(1); prob_transpose(4); fill(1); scores(5)
            attend(4); xc_transpose(2, 6); values_out(5); fill(1); gate(2); fill(1); prob_transpose(5)
            xc_transpose(3, 6); fill(1); attend(5); gate(3); fill(4); xc_transpose(4, 6); fill(2); gate(4)
            fill(4); xc_transpose(5, 6); fill(1); gate(5)
            pe.wait_ge(prob_ready, TILES)
            pe.wait_ge(Gimg_ready, 1)
            for t in range(EARLY):
                image_gates(t)
            fill(WARM_GATE)
            for t in range(EARLY, TILES):
                pe.wait_ge(Gimg_ready, 1 + t - EARLY + 1)
                image_gates(t)
            fill(WARM_TOPK)
            pe.wait_ge(slotT_ready, 1)
            pe.wait_ge(identb_ready, 1)
            nc.tensor.matmul(bank[TOP_BANK][0:P, 128:128 + RT], slotT[:, :, :].rearrange("r b s -> r (b s)"),
                             identb[:, :], start=True, stop=True).then_inc(slot_mm, 1)
            fill(WARM_PICK)

            pe.wait_ge(xlo_ready, len(GROUPS))
            for h in range(2):
                for t in range(TILES):
                    if t in FIRST_PICKED:
                        pe.wait_ge(pick_ready, h * len(PICKS) + FIRST_PICKED.index(t) + 1)
                    w = EH * NB[t] * TOPK
                    c0 = (t % EX_TILES) * EH * SL
                    for part in range(3):
                        last = nc.tensor.matmul(bank[EX_BANK[h][t // EX_TILES]][:, c0:c0 + w],
                                                xpart[0:NT[t], part, t, :],
                                                pick[0:NT[t], half_cols(t, h, NB[t] * TOPK)],
                                                start=part == 0, stop=part == 2)
                    if t in (EX_TILES - 1, TILES - 1):
                        last.then_inc(ex_mm, 1)

            pe.wait_ge(in_w1, 16)
            pe.wait_ge(ex_sb, 1)
            pe.wait_ge(ex_sb_act, 1)
            for k in range(HID_BANKS):
                k0, kn = PER_BANK * k, min(PER_BANK, EC - PER_BANK * k)
                hb_ = bank[HID_BANK[k]]
                for ec in range(k0, k0 + kn):
                    e, c = ec // FCH, ec % FCH
                    if e == EH and c == 0:
                        pe.wait_ge(ex_sb, 2)
                        pe.wait_ge(ex_sb_act, 2)
                    last = nc.tensor.matmul(hb_[:, (ec - k0) * NS:(ec - k0 + 1) * NS],
                                            w1s[:, e, c * 128:(c + 1) * 128], exT[:, e, :], start=True, stop=True)
                last.then_inc(hid_mm, 1)

            pe.wait_ge(wpick_ready, 1)
            for p in range(PAIRS):
                pe.wait_ge(hid_sb, min(PER_BANK * (HID_BANK.index(PUT_BANK[p]) + 1), EC))
                for t in (2 * p, 2 * p + 1):
                    n, w = NT[t], NB[t] * TOPK
                    for h in range(2):
                        at_col = ((t % 2) * 2 + h) * P
                        last = nc.tensor.transpose(bank[PUT_BANK[p]][0:EH * w, at_col:at_col + n],
                                                   wpick[0:n, half_cols(t, h, w)], ident[0:n, 0:n])
                last.then_inc(put_mm, 1)

            pe.wait_ge(in_w2, 16)
            for j in range(Y_BANKS):
                e0, k = PER_BANK * j, min(PER_BANK, E - PER_BANK * j)
                for e in range(e0, e0 + k):
                    for c in range(FCH):
                        ec = FCH * e + c
                        pe.wait_ge(hid_sb, ec + 1)
                        last = nc.tensor.matmul(bank[Y_BANK[j]][:, (e - e0) * NS:(e - e0 + 1) * NS],
                                                w2s[:, e, c, :], hid[:, ec * NS:(ec + 1) * NS],
                                                start=c == 0, stop=c == FCH - 1)
                last.then_inc(y_mm, 1)

            pe.wait_ge(hid_sb, EC)
            pe.wait_ge(put_sb, PAIRS)
            for h in range(2):
                if h == 0:
                    pe.wait_ge(yT_sb, 2)
                else:
                    pe.wait_ge(yT_sb, Y_BANKS)
                for t in range(TILES):
                    w = NB[t] * TOPK
                    last = nc.tensor.transpose(bank[YT_BANK[t]][0:EH * w, h * D:(h + 1) * D],
                                               yT[:, half_cols(t, h, w)], ident[:, :])
                    if h == 1:
                        last.then_inc(yt_mm, 1)

            for t in range(TILES):
                w = EH * NB[t] * TOPK
                if t % 2 == 0:
                    pe.wait_ge(y_sb, t // 2 + 1)
                else:
                    pe.wait_ge(y_sb_act, t // 2 + 1)
                if t == 4:
                    pe.wait_ge(y_sb, TILES // 2)
                if t == 5:
                    pe.wait_ge(y_sb_act, TILES // 2)
                for h in range(2):
                    last = nc.tensor.matmul(bank[RES_BANK[t]][0:NT[t], 0:D], put[0:w, 2 * t + h, 0:NT[t]],
                                            y[0:w, 2 * t + h, :], start=h == 0, stop=h == 1)
                last.then_inc(res_mm, 1)


def kernel(x, cls_tok, L0_tok_w, L0_tok_b, L0_attn_Wq, L0_attn_bq, L0_attn_Wk, L0_attn_bk, L0_attn_Wv, L0_attn_bv,
           L0_attn_Wo, L0_attn_bo, L0_attn_gamma, L0_attn_beta, L0_ffn_Wg, L0_ffn_W1, L0_ffn_b1, L0_ffn_W2, L0_ffn_b2):
    import concourse.bacc as bacc
    from concourse.bass_utils import run_bass_kernel_spmd

    px = np.asarray(x).reshape(B, C, HP, PATCH, HP, PATCH).transpose(1, 3, 5, 0, 2, 4).reshape(KCH, 128, B, S - 1)
    full = np.zeros((KCH, 128, B, S), np.float32)
    full[:, :, :, 1:] = px
    full = full.transpose(1, 0, 2, 3)
    patches = np.concatenate([full[:, :, TILE_B * t:TILE_B * t + NB[t]].reshape(128, KCH * NT[t])
                              for t in range(TILES)], axis=1)
    w_tok = np.asarray(L0_tok_w).reshape(D, KCH, 128).transpose(2, 1, 0).reshape(128, KCH * D)
    rows = np.concatenate([np.asarray(a).reshape(-1, D) for a in (
        L0_tok_b, cls_tok, L0_attn_bo)])
    const_f, const_h, part = constants()
    bias_rows = np.concatenate([np.repeat(rows, 3, axis=0), part], axis=1)
    feature_biases = np.concatenate([np.asarray(a).reshape(-1, 128) for a in (L0_attn_bq, L0_attn_bk, L0_attn_bv)]
                                    + [np.asarray(L0_ffn_b1).reshape(EC, 128), np.asarray(L0_ffn_b2)]).T
    w_qkvo = np.concatenate([np.asarray(a) for a in (L0_attn_Wq, L0_attn_Wk, L0_attn_Wv, L0_attn_Wo)], axis=1)
    arrays = {
        "patches": patches, "w_tok": w_tok, "bias_rows": bias_rows, "feature_biases": feature_biases,
        "const_f": const_f, "const_h": const_h,
        "w_qkvo": w_qkvo, "w_gate": np.asarray(L0_ffn_Wg), "gamma": np.asarray(L0_attn_gamma),
        "beta": np.asarray(L0_attn_beta), "w1": np.asarray(L0_ffn_W1).transpose(1, 0, 2),
        "w2": np.asarray(L0_ffn_W2).reshape(E, FCH, 128, D).transpose(2, 0, 1, 3),
    }
    arrays = {name: np.ascontiguousarray(a) for name, a in arrays.items()}
    nc = bacc.Bacc("TRN2", target_bir_lowering=False, num_devices=1)
    args = [nc.dram_tensor(name, a.shape, mybir.dt.float32, kind="ExternalInput").ap() for name, a in arrays.items()]
    out = nc.dram_tensor("out", (B * S, D), mybir.dt.float32, kind="ExternalOutput").ap()
    vit_block(nc, *args, out)
    r = run_bass_kernel_spmd(nc, [arrays], core_ids=[0])
    return r.results[0]["out"].reshape(B, S, D)
```
